# Optimizing a Trainium2 kernel written in Bass

```python
import numpy as np
import jax
import jax.numpy as jnp

def _softmax(x, axis=-1):
    return jax.nn.softmax(x, axis=axis)

def _gelu(x):
    return jax.nn.gelu(x, approximate=True)

def _silu(x):
    return jax.nn.silu(x)

def _sigmoid(x):
    return jax.nn.sigmoid(x)

def _layernorm(x, axis=-1, eps=1e-05):
    m = jnp.mean(x, axis=axis, keepdims=True)
    v = jnp.var(x, axis=axis, keepdims=True)
    return (x - m) / jnp.sqrt(v + eps)

def _scatter_add(tgt, idx, src, axis=0):
    return tgt.at[idx].add(src)

def _segment_sum(src, seg, n):
    return jax.ops.segment_sum(src, seg, n)
kernel_name = 'mk_flamingo_gated_d1_seqx_r8_c1d5ba'

def setup_inputs(seed: int=0):
    np.random.seed(seed)
    _w = jnp.asarray

    def _rec_inputs():
        import jax
        import jax.numpy as jnp
        _rk = jax.random.key(seed)
        x = 7.22e-05 + 1 * jax.random.normal(jax.random.fold_in(_rk, 1), (16, 128, 128), jnp.float32)
        _lenS = 128 - jax.random.randint(jax.random.fold_in(_rk, 7), (16,), 0, max(1, 128 // 4) + 1, jnp.int32)
        _lenS2 = 77 - jax.random.randint(jax.random.fold_in(_rk, 8), (16,), 0, max(1, 77 // 4) + 1, jnp.int32)
        _ctx_768P = jax.random.normal(jax.random.fold_in(_rk, 11), (16, 16, 96), jnp.float32)
        _ctx_768c = jax.random.dirichlet(jax.random.fold_in(_rk, 511), 0.3 * jnp.ones((16,), jnp.float32), (16, 77))
        _ctx_768t = jnp.einsum('bsk,bkd->bsd', _ctx_768c, _ctx_768P)
        _ctx_768t = _ctx_768t * jax.lax.rsqrt(jnp.mean(jnp.square(_ctx_768t)) + 1e-12) * 0.953939
        ctx_768 = -0.000191848 + 0.999787 * (_ctx_768t + 0.3 * jax.random.normal(jax.random.fold_in(_rk, 611), (16, 77, 96), jnp.float32))
        _g = jax.random.normal(jax.random.fold_in(_rk, 9001), (2, 1), jnp.float32)
        _g = jnp.sign(_g) * jnp.maximum(jnp.abs(_g), 1.0) + (_g == 0) * 1.0
        g_xattn = _g[0]
        g_ffn = _g[1]
        return (x, ctx_768, g_xattn, g_ffn)
    x, ctx_768, g_xattn, g_ffn = _rec_inputs()

    def _L0_xattn_setup():
        import jax, jax.numpy as jnp
        import numpy as np
        N_HEADS = 16
        key = jax.random.key(seed)
        ks = jax.random.split(key, 8)
        b, l, m = (8, 128, 128)
        d_embed, d_cross = (128, 96)
        s_q = 1.0 / np.sqrt(d_embed)
        s_kv = 1.0 / np.sqrt(d_cross)
        return {'x': jax.random.normal(ks[0], (b, l, d_embed), jnp.float32), 'y': jax.random.normal(ks[1], (b, m, d_cross), jnp.float32), 'Wq': jax.random.normal(ks[2], (d_embed, d_embed), jnp.float32) * s_q, 'bq': jax.random.normal(ks[3], (d_embed,), jnp.float32) * 0.01, 'Wkv': jax.random.normal(ks[4], (2 * d_embed, d_cross), jnp.float32) * s_kv, 'bkv': jax.random.normal(ks[5], (2 * d_embed,), jnp.float32) * 0.01, 'Wo': jax.random.normal(ks[6], (d_embed, d_embed), jnp.float32) * s_q, 'bo': jax.random.normal(ks[7], (d_embed,), jnp.float32) * 0.01}
    _L0_xattn_all = _L0_xattn_setup()
    _L0_xattn_in = {k: v for k, v in _L0_xattn_all.items() if k in ('Wq', 'bq', 'Wkv', 'bkv', 'Wo', 'bo')}
    del _L0_xattn_all

    def _L0_ffn_setup():
        import jax, jax.numpy as jnp
        import numpy as np
        B, S, H, F, E, R, TOPK = (4, 256, 128, 512, 4, 4, 2)

        def _more_forward(x, Wg, bg, W1, b1, W2, b2):
            b, s, h = x.shape
            cur = x
            for r in range(R):
                flat = cur.reshape(-1, h)
                logits = flat @ Wg[r] + bg[r]
                vals, idx = jax.lax.top_k(logits, TOPK)
                w = jax.nn.softmax(vals, axis=-1)
                cw = jnp.sum(jax.nn.one_hot(idx, E, dtype=flat.dtype) * w[..., None], axis=1)
                hmid = jax.nn.gelu(jnp.einsum('nh,ehf->enf', flat, W1) + b1[:, None, :])
                y = jnp.einsum('enf,efh->enh', hmid, W2) + b2[:, None, :]
                out = jnp.einsum('ne,enh->nh', cw, y)
                cur = cur + out.reshape(b, s, h)
            return cur
        key = jax.random.key(seed)
        ks = jax.random.split(key, 8)
        scale = 0.02
        return {'x': jax.random.normal(ks[0], (B, S, H), dtype=jnp.float32), 'Wg': jax.random.normal(ks[1], (R, H, E), dtype=jnp.float32) * scale, 'bg': jnp.zeros((R, E), dtype=jnp.float32), 'W1': jax.random.normal(ks[2], (E, H, F), dtype=jnp.float32) * scale, 'b1': jnp.zeros((E, F), dtype=jnp.float32), 'W2': jax.random.normal(ks[3], (E, F, H), dtype=jnp.float32) * scale, 'b2': jnp.zeros((E, H), dtype=jnp.float32)}
    _L0_ffn_all = _L0_ffn_setup()
    _L0_ffn_in = {k: v for k, v in _L0_ffn_all.items() if k in ('Wg', 'bg', 'W1', 'b1', 'W2', 'b2')}
    del _L0_ffn_all
    return {'x': x, 'ctx_768': ctx_768, 'g_xattn': g_xattn, 'g_ffn': g_ffn, 'L0_xattn_Wq': _L0_xattn_in['Wq'], 'L0_xattn_bq': _L0_xattn_in['bq'], 'L0_xattn_Wkv': _L0_xattn_in['Wkv'], 'L0_xattn_bkv': _L0_xattn_in['bkv'], 'L0_xattn_Wo': _L0_xattn_in['Wo'], 'L0_xattn_bo': _L0_xattn_in['bo'], 'L0_ffn_Wg': _L0_ffn_in['Wg'], 'L0_ffn_bg': _L0_ffn_in['bg'], 'L0_ffn_W1': _L0_ffn_in['W1'], 'L0_ffn_b1': _L0_ffn_in['b1'], 'L0_ffn_W2': _L0_ffn_in['W2'], 'L0_ffn_b2': _L0_ffn_in['b2']}

def reference(x, ctx_768, g_xattn, g_ffn, L0_xattn_Wq, L0_xattn_bq, L0_xattn_Wkv, L0_xattn_bkv, L0_xattn_Wo, L0_xattn_bo, L0_ffn_Wg, L0_ffn_bg, L0_ffn_W1, L0_ffn_b1, L0_ffn_W2, L0_ffn_b2):
    import jax
    import jax.numpy as jnp

    def _L0_xattn_ref(x, y, Wq, bq, Wkv, bkv, Wo, bo):
        import jax, jax.numpy as jnp
        import numpy as np
        N_HEADS = 16
        b, l, d = x.shape
        m = y.shape[1]
        h = N_HEADS
        dh = d // h
        q = (jnp.einsum('bld,ed->ble', x, Wq) + bq).reshape(b, l, h, dh)
        kv = (jnp.einsum('bmc,ec->bme', y, Wkv) + bkv).reshape(b, m, h, 2 * dh)
        k, v = (kv[..., :dh], kv[..., dh:])
        scale = 1.0 / jnp.sqrt(jnp.asarray(dh, x.dtype))
        att = jax.nn.softmax(jnp.einsum('blhd,bmhd->blmh', q, k) * scale, axis=2)
        out = jnp.einsum('blmh,bmhd->blhd', att, v).reshape(b, l, d)
        return jnp.einsum('bld,ed->ble', out, Wo) + bo

    def _L0_ffn_ref(x, Wg, bg, W1, b1, W2, b2):
        import jax, jax.numpy as jnp
        import numpy as np
        B, S, H, F, E, R, TOPK = (4, 256, 128, 512, 4, 4, 2)

        def _more_forward(x, Wg, bg, W1, b1, W2, b2):
            b, s, h = x.shape
            cur = x
            for r in range(R):
                flat = cur.reshape(-1, h)
                logits = flat @ Wg[r] + bg[r]
                vals, idx = jax.lax.top_k(logits, TOPK)
                w = jax.nn.softmax(vals, axis=-1)
                cw = jnp.sum(jax.nn.one_hot(idx, E, dtype=flat.dtype) * w[..., None], axis=1)
                hmid = jax.nn.gelu(jnp.einsum('nh,ehf->enf', flat, W1) + b1[:, None, :])
                y = jnp.einsum('enf,efh->enh', hmid, W2) + b2[:, None, :]
                out = jnp.einsum('ne,enh->nh', cw, y)
                cur = cur + out.reshape(b, s, h)
            return cur
        return _more_forward(x, Wg, bg, W1, b1, W2, b2)
    x = x + jnp.tanh(g_xattn[0]) * _L0_xattn_ref(_layernorm(x, axis=-1), ctx_768, L0_xattn_Wq, L0_xattn_bq, L0_xattn_Wkv, L0_xattn_bkv, L0_xattn_Wo, L0_xattn_bo)
    x = x + jnp.tanh(g_ffn[0]) * _L0_ffn_ref(_layernorm(x, axis=-1), L0_ffn_Wg, L0_ffn_bg, L0_ffn_W1, L0_ffn_b1, L0_ffn_W2, L0_ffn_b2)
    return x

_drawn_inputs = setup_inputs


def setup_inputs(seed=0):
    import zlib

    import numpy as np

    out = dict(_drawn_inputs(seed))
    spreads = {'L0_ffn_bg': (0.0, 0.1), 'L0_ffn_b1': (0.0, 0.1), 'L0_ffn_b2': (0.0, 0.1)}
    factors = {'L0_xattn_bq': 4.382}
    for name, (base, spread) in spreads.items():
        noise = np.random.default_rng([zlib.crc32(name.encode()), seed]).standard_normal(out[name].shape)
        drawn = base * np.exp(spread * noise) if base else spread * noise
        out[name] = jnp.asarray(drawn.astype(out[name].dtype))
    for name, factor in factors.items():
        out[name] = (out[name] * factor).astype(out[name].dtype)
    return out
```

```python
from contextlib import ExitStack

import concourse.bass as bass
from concourse import mybir

P = 128
F32 = mybir.dt.float32
F32R = mybir.dt.float32r
ALU = mybir.AluOpType
ACT = mybir.ActivationFunctionType
AX = mybir.AxisListType
EPS = 1e-5


def flamingo_gated_block(
    nc: bass.Bass,
    x: bass.AP,
    ctx_in: bass.AP,
    g_xattn: bass.AP,
    g_ffn: bass.AP,
    Wq: bass.AP,
    bq: bass.AP,
    Wkv: bass.AP,
    bkv: bass.AP,
    Wo: bass.AP,
    bo: bass.AP,
    Wg: bass.AP,
    bg: bass.AP,
    W1: bass.AP,
    b1: bass.AP,
    W2: bass.AP,
    b2: bass.AP,
    out: bass.AP,
):
    B, L, D = x.shape
    M, C = ctx_in.shape[1:]
    ROUNDS, _, E = Wg.shape
    F = W1.shape[2]
    H = 16
    DH = D // H
    SCALE = float(DH) ** -0.5
    HQ = 32 // DH
    NQ = P // 32
    VW = DH + 1
    N = B * L
    CH = 512
    NC = N // CH
    TC = CH // P
    NF = F // P
    BG = B // TC
    STEPS = ROUNDS * NC
    HM = HQ * M
    GATE_OPS = 11
    assert L == P and D == P and H == HQ * NQ and N % CH == 0 and F == NF * P and B % TC == 0
    assert M <= P and C <= P and TC * M <= CH and F == CH and NF == 4 and STEPS == B

    with ExitStack() as stack:
        def sb(name, shape, dt=F32):
            return stack.enter_context(nc.sbuf_tensor(name, shape, dt))

        def sem(name):
            return stack.enter_context(nc.semaphore(name))

        ps = stack.enter_context(nc.psum_tensor("ps", [P, 8, CH], F32))

        ident = sb("ident", [P, P])
        head_at = sb("head_at", [P, NQ, HQ])
        head_mask = sb("head_mask", [P, HQ])
        before = sb("before", [P, E, E])
        after = sb("after", [P, E, E])
        minus_half = sb("minus_half", [P, B])
        gates = sb("gates", [P, 2])
        tgates = sb("tgates", [P, 2])
        NCOL = E * NF + E + 2
        rows_in = sb("rows_in", [NCOL, P])
        cols = sb("cols", [P, NCOL])
        b1_c = cols[:, 0:E * NF]
        b2_c = cols[:, E * NF:E * NF + E]
        bq_c = cols[:, NCOL - 2:NCOL - 1]
        bk_c = cols[:, NCOL - 1:NCOL]
        bv_row = sb("bv_row", [P, D])
        bo_row = sb("bo_row", [P, D])
        bg_row = sb("bg_row", [P, ROUNDS * E])
        wq_in = sb("wq_in", [P, D])
        wk_in = sb("wk_in", [P, C])
        wv_in = sb("wv_in", [P, C])
        wo_in = sb("wo_in", [P, D])
        wT = sb("wT", [P, 4, P])
        wg_in = sb("wg_in", [P, ROUNDS, E])
        wg_s = sb("wg_s", [P, ROUNDS, 2, E], F32R)
        w1_in = sb("w1_in", [P, E * F])
        w2_in = sb("w2_in", [P, E * NF * D])
        w1_hi = sb("w1_hi", [P, E * F], F32R)
        w1_lo = sb("w1_lo", [P, E * F], F32R)
        w2_hi = sb("w2_hi", [P, E * NF * D], F32R)
        w2_lo = sb("w2_lo", [P, E * NF * D], F32R)
        x_sb = sb("x_sb", [P, B, D])
        xres = sb("xres", [P, B, D])
        x1_sb = x_sb
        stats = sb("stats", [P, B, 6])
        mv = sb("mv", [P, B, 2])
        veps = sb("veps", [P, B])
        rstd = sb("rstd", [P, B])
        xn = sb("xn", [P, B, D])
        ctx_sb = sb("ctx_sb", [M, B, C])
        ctxT = sb("ctxT", [C, B * M])
        xnT = sb("xnT", [P, N])
        qT = sb("qT", [P, N])
        kT = sb("kT", [P, B * M])
        vaug = sb("vaug", [M, B, H, VW])
        q_hi = sb("q_hi", [P, L], F32R)
        q_lo = sb("q_lo", [P, L], F32R)
        k_f = sb("k_f", [P, HQ, M])
        k_hi = sb("k_hi", [P, HQ * M], F32R)
        k_lo = sb("k_lo", [P, HQ * M], F32R)
        v_st = sb("v_st", [M, H * VW])
        prob = sb("prob", [P, NQ, HM])
        probT = sb("probT", [M, NQ, HQ * L])
        mx = sb("mx", [P, H])
        rden = sb("rden", [P, H])
        o_n = sb("o_n", [P, D])
        oT_sb = sb("oT_sb", [P, L])
        cur = sb("cur", [P, N])
        x_hi = sb("x_hi", [P, CH], F32R)
        x_lo = sb("x_lo", [P, CH], F32R)
        g_sb = sb("g_sb", [P, NF, CH])
        h_hi = sb("h_hi", [P, 2, NF, CH], F32R)
        h_lo = sb("h_lo", [P, 2, NF, CH], F32R)
        cwb_sb = sb("cwb_sb", [P, 2, CH])
        contrib = sb("contrib", [P, 2, CH])
        lga = sb("lga", [P, TC, E])
        lg = sb("lg", [P, TC, E])
        beat_ge = sb("beat_ge", [P, TC, E, E])
        beat_gt = sb("beat_gt", [P, TC, E, E])
        rank = sb("rank", [P, TC, E])
        sel_lg = sb("sel_lg", [P, TC, E])
        sel_sum = sb("sel_sum", [P, TC])
        half_d = sb("half_d", [P, TC, E])
        th = sb("th", [P, TC, E])
        wgt = sb("wgt", [P, TC, E])
        cw = sb("cw", [P, TC, E])
        out_sb = xn

        x_in = [sem(f"x_in{c}") for c in range(BG)]
        ctx_ld = sem("ctx_ld")
        wproj_ld = sem("wproj_ld")
        small_ld = sem("small_ld")
        rows_ld = sem("rows_ld")
        gates_ld = sem("gates_ld")
        moe_ld = sem("moe_ld")
        out_st = sem("out_st")
        c_zero = sem("c_zero")
        c_mask = sem("c_mask")
        c_ready = sem("c_ready")
        cols_ready = sem("cols_ready")
        headmask_ready = sem("headmask_ready")
        tg_ready = sem("tg_ready")
        ones_ready = sem("ones_ready")
        bn_step = sem("bn_step")
        mv_ready = sem("mv_ready")
        veps_ready = sem("veps_ready")
        rstd_ready = sem("rstd_ready")
        xn_ready = sem("xn_ready")
        xres_step = sem("xres_step")
        pre_mm = sem("pre_mm")
        pre_act = sem("pre_act")
        pre_dve = sem("pre_dve")
        k_stage = sem("k_stage")
        v_stage = sem("v_stage")
        q_stage = sem("q_stage")
        w_split = sem("w_split")
        scores_done = sem("scores_done")
        mx_done = sem("mx_done")
        sub_done = sem("sub_done")
        exp_done = sem("exp_done")
        pt_done = sem("pt_done")
        pt_moved = sem("pt_moved")
        pv_done = sem("pv_done")
        rden_done = sem("rden_done")
        on_done = sem("on_done")
        oT_done = sem("oT_done")
        oT_moved = sem("oT_moved")
        wo_done = sem("wo_done")
        x1_done = sem("x1_done")
        st_done = sem("st_done")
        curT_done = sem("curT_done")
        cur_ready = sem("cur_ready")
        wg_split = sem("wg_split")
        x_hi_done = sem("x_hi_done")
        x_split = sem("x_split")
        logits_done = sem("logits_done")
        gate_step = sem("gate_step")
        th_done = sem("th_done")
        wgt_done = sem("wgt_done")
        cw_ready = sem("cw_ready")
        w1_done = sem("w1_done")
        gelu_done = sem("gelu_done")
        hi_act = sem("hi_act")
        hi_dve = sem("hi_dve")
        lo_done = sem("lo_done")
        y_done = sem("y_done")
        y_read = sem("y_read")
        cwb_done = sem("cwb_done")
        cwb_moved = sem("cwb_moved")
        fin_mm = sem("fin_mm")
        fin_done = sem("fin_done")

        SC = 0
        TB = 4
        OB = ps[:, 6, 0:H * VW]
        OT = ps[:, 7, 0:L]
        AO = ps[:, 7, L:L + D]
        YB = 4
        CWB = ps[:, 6, :]
        LG = ps[:, 7, 0:TC * ROUNDS * 2 * E]
        LG_N = ROUNDS * 2 * E

        J_W, J_CTX, J_K, J_V = 0, 1, 1 + BG, 1 + 2 * BG
        J_XN, J_Q = 1 + 3 * BG, 1 + 4 * BG
        JOBS = 1 + 5 * BG
        on_dve = [J_V <= j < J_Q for j in range(JOBS)]

        def moved(eng, j):
            n = sum(d == on_dve[j] for d in on_dve[:j + 1])
            eng.wait_ge(pre_dve if on_dve[j] else pre_act, n)

        def bank(j):
            return ps[:, j % 8, :]

        COLS = bank(J_CTX)[:, TC * M:TC * M + NCOL]

        x_v = x.rearrange("b l d -> l b d")
        out_v = out.rearrange("b l d -> l b d")
        kv_v = Wkv.rearrange("(h t d) c -> t h d c", h=H, t=2)
        bkv_v = bkv.rearrange("(h t d) -> t h d", h=H, t=2)

        block = stack.enter_context(nc.Block())

        @block.sync
        def _(sp):
            sp.dma_start(wq_in[:, :], Wq).then_inc(wproj_ld, 16)
            sp.dma_start(wk_in[:, :], kv_v[0].rearrange("h d c -> h d c")).then_inc(wproj_ld, 16)
            sp.dma_start(wv_in[:, :], kv_v[1].rearrange("h d c -> h d c")).then_inc(wproj_ld, 16)
            sp.dma_start(wo_in[:, :], Wo).then_inc(wproj_ld, 16)
            for c in range(BG):
                sp.dma_start(x_sb[:, TC * c:TC * c + TC, :],
                             x_v[:, TC * c:TC * c + TC, :]).then_inc(x_in[c], 16)
            sp.dma_start(wg_in[:, :, :], Wg.rearrange("r h e -> h r e")).then_inc(moe_ld, 16)
            sp.dma_start(w1_in[:, :].rearrange("h (e f) -> h e f", e=E),
                         W1.rearrange("e h f -> h e f")).then_inc(moe_ld, 16)
            sp.dma_start(w2_in[:, :].rearrange("p (e k h) -> p e k h", e=E, k=NF),
                         W2.rearrange("e (k p) h -> p e k h", p=P)).then_inc(moe_ld, 16)
            for c in range(NC):
                sp.wait_ge(fin_done, c + 1)
                sp.dma_start(out_v[:, TC * c:TC * c + TC, :],
                             out_sb[:, TC * c:TC * c + TC, :]).then_inc(out_st, 16)
            sp.wait_ge(out_st, 16 * NC)

        @block.gpsimd
        def _(pool):
            nc.gpsimd.memset(ident[:, :], 0.0).then_inc(c_zero, 1)
            nc.gpsimd.memset(head_at[:, :, :], 1.0).then_inc(c_zero, 1)
            nc.gpsimd.memset(before[:, :, :], 1.0).then_inc(c_zero, 1)
            nc.gpsimd.memset(after[:, :, :], 1.0).then_inc(c_zero, 1)
            nc.gpsimd.memset(minus_half[:, :], -0.5).then_inc(c_zero, 1)
            pool.wait_ge(c_zero, 5)
            nc.gpsimd.affine_select(out=ident[:, :], in_=ident[:, :], compare_op=ALU.not_equal, fill=1.0,
                                    base=0, pattern=[[-1, P]], channel_multiplier=1).then_inc(c_ready, 1)
            nc.gpsimd.affine_select(out=head_at[:, :, :], in_=head_at[:, :, :], compare_op=ALU.is_ge, fill=0.0,
                                    base=0, pattern=[[-32, NQ], [-DH, HQ]],
                                    channel_multiplier=1).then_inc(c_mask, 1)
            pool.wait_ge(c_mask, 1)
            nc.gpsimd.affine_select(out=head_at[:, :, :], in_=head_at[:, :, :], compare_op=ALU.is_ge, fill=0.0,
                                    base=DH - 1, pattern=[[32, NQ], [DH, HQ]],
                                    channel_multiplier=-1).then_inc(c_ready, 1)
            nc.gpsimd.affine_select(out=before[:, :, :], in_=before[:, :, :], compare_op=ALU.is_ge, fill=0.0,
                                    base=-1, pattern=[[1, E], [-1, E]], channel_multiplier=0).then_inc(c_ready, 1)
            nc.gpsimd.affine_select(out=after[:, :, :], in_=after[:, :, :], compare_op=ALU.is_ge, fill=0.0,
                                    base=-1, pattern=[[-1, E], [1, E]], channel_multiplier=0).then_inc(c_ready, 1)

            def rstd_of(n):
                pool.wait_ge(mv_ready, B * n)
                nc.gpsimd.tensor_scalar(veps[:, :], mv[:, :, 1], EPS, None, ALU.add).then_inc(veps_ready, 1)
                pool.wait_ge(veps_ready, n)
                nc.gpsimd.tensor_tensor(rstd[:, :], veps[:, :], minus_half[:, :], ALU.pow).then_inc(rstd_ready, 1)

            rstd_of(1)
            headm = head_mask[:, :].unsqueeze(2).to_broadcast([P, HQ, M])

            def stage_k(b):
                pool.wait_ge(scores_done, b)
                pool.wait_ge(k_stage, 3 * b)
                kb = kT[:, bass.ds(b * M, M)].unsqueeze(1).to_broadcast([P, HQ, M])
                nc.gpsimd.tensor_tensor(k_f[:, :, :], kb, headm, ALU.mult).then_inc(k_stage, 1)
                nc.gpsimd.tensor_tensor(k_hi[:, :].rearrange("p (h m) -> p h m", m=M), kb, headm,
                                        ALU.mult).then_inc(k_stage, 1)
                pool.wait_ge(k_stage, 3 * b + 2)
                nc.gpsimd.tensor_tensor(k_lo[:, :], k_f[:, :, :].rearrange("p h m -> p (h m)"), k_hi[:, :].bitcast(F32),
                                        ALU.subtract).then_inc(k_stage, 1)

            def stage_v(b):
                pool.wait_ge(pv_done, NQ * b + NQ)
                nc.gpsimd.tensor_copy(v_st[:, :],
                                      vaug[:, :, :, :].rearrange("m b h v -> m (b h v)")
                                      [:, bass.ds(b * (H * VW), H * VW)]).then_inc(v_stage, 1)

            WS = E * F // B

            def split_w(b):
                s = bass.ds(b * WS, WS)
                nc.gpsimd.tensor_copy(w1_hi[:, s], w1_in[:, s]).then_inc(w_split, 1)
                nc.gpsimd.tensor_copy(w2_hi[:, s], w2_in[:, s]).then_inc(w_split, 1)
                pool.wait_ge(w_split, 4 * b + 2)
                nc.gpsimd.tensor_tensor(w1_lo[:, s], w1_in[:, s], w1_hi[:, s].bitcast(F32),
                                        ALU.subtract).then_inc(w_split, 1)
                nc.gpsimd.tensor_tensor(w2_lo[:, s], w2_in[:, s], w2_hi[:, s].bitcast(F32),
                                        ALU.subtract).then_inc(w_split, 1)

            pool.wait_ge(headmask_ready, 1)
            moved(pool, J_K + BG - 1)
            stage_k(0)
            pool.wait_ge(tg_ready, 1)
            pool.wait_ge(small_ld, 16 * 3)
            nc.gpsimd.tensor_scalar(bo_row[:, :], bo_row[:, :], tgates[:, 0:1], None,
                                    ALU.mult).then_inc(xres_step, 1)
            pool.wait_ge(xres_step, 1)
            for c in range(BG):
                pool.wait_ge(x_in[c], 16)
            nc.gpsimd.tensor_tensor(xres[:, :, :], x_sb[:, :, :],
                                    bo_row[:, :].unsqueeze(1).to_broadcast([P, B, D]),
                                    ALU.add).then_inc(xres_step, 1)
            pool.wait_ge(moe_ld, 16 * 3)
            moved(pool, J_V + BG - 1)
            with pool.Fori(0, B - 1) as b:
                stage_k(b + 1)
                stage_v(b)
                split_w(b)
            stage_v(B - 1)
            split_w(B - 1)

            rstd_of(2)

            UNITS = STEPS * E

            share_v = contrib[:, :, :].rearrange("p s n -> p (s n)")
            with pool.Fori(0, UNITS) as u:
                pool.wait_ge(y_read, u + 3)
                pool.wait_ge(cur_ready, u + B)
                cc = cur[:, bass.ds(((u // E) % NC) * CH, CH)]
                nc.gpsimd.tensor_tensor(cc, cc, share_v[:, bass.ds((u % 2) * CH, CH)],
                                        ALU.add).then_inc(cur_ready, 1)

        @block.scalar
        def _(act):
            act.dma_start(ctx_sb[:, :, :], ctx_in.rearrange("b m c -> m b c")).then_inc(ctx_ld, 16)
            act.dma_start(gates[:, 0:1], g_xattn.rearrange("(o a) -> o a", o=1).to_broadcast([P, 1])).then_inc(gates_ld, 16)
            act.dma_start(gates[:, 1:2], g_ffn.rearrange("(o a) -> o a", o=1).to_broadcast([P, 1])).then_inc(gates_ld, 16)
            act.dma_start(rows_in[0:E * NF, :], b1.rearrange("e (k p) -> (e k) p", p=P)).then_inc(rows_ld, 16)
            act.dma_start(rows_in[E * NF:E * NF + E, :], b2).then_inc(rows_ld, 16)
            act.dma_start(rows_in[NCOL - 2:NCOL - 1, :], bq.unsqueeze(0)).then_inc(rows_ld, 16)
            act.dma_start(rows_in[NCOL - 1:NCOL, :].rearrange("o (h d) -> o h d", h=H),
                          bkv_v[0].unsqueeze(0)).then_inc(rows_ld, 16)
            act.dma_start(bv_row[:, :].rearrange("p (h d) -> p h d", h=H),
                          bkv_v[1].unsqueeze(0).to_broadcast([P, H, DH])).then_inc(small_ld, 16)
            act.dma_start(bo_row[:, :], bo.unsqueeze(0).to_broadcast([P, D])).then_inc(small_ld, 16)
            act.dma_start(bg_row[:, :], bg.rearrange("r e -> (r e)").unsqueeze(0)
                          .to_broadcast([P, ROUNDS * E])).then_inc(small_ld, 16)
            act.sem_inc(gelu_done, NF)
            act.sem_inc(pt_moved, 2)
            act.sem_inc(cwb_moved, 1)
            act.wait_ge(gates_ld, 32)
            nc.scalar.activation(tgates[:, :], gates[:, :], ACT.Tanh).then_inc(tg_ready, 1)

            act.wait_ge(small_ld, 16 * 3)
            act.wait_ge(pre_mm, J_W + 1)
            nc.scalar.activation(wT[:, 0, :], bank(J_W)[:, 0:P], ACT.Copy)
            nc.scalar.activation(wT[0:C, 1:3, :], bank(J_W)[0:C, P:3 * P].rearrange("p (a b) -> p a b", a=2), ACT.Copy)
            nc.scalar.activation(wT[:, 3, :], bank(J_W)[:, 3 * P:4 * P], ACT.Copy).then_inc(pre_act, 1)
            act.wait_ge(pre_mm, J_CTX + 1)
            nc.scalar.activation(cols[:, :], COLS, ACT.Copy).then_inc(cols_ready, 1)
            act.wait_ge(cols_ready, 1)
            for c in range(BG):
                act.wait_ge(pre_mm, J_CTX + c + 1)
                nc.scalar.activation(ctxT[:, TC * M * c:TC * M * (c + 1)], bank(J_CTX + c)[0:C, 0:TC * M],
                                     ACT.Copy).then_inc(pre_act, 1)
            for c in range(BG):
                act.wait_ge(pre_mm, J_K + c + 1)
                nc.scalar.activation(kT[:, TC * M * c:TC * M * (c + 1)], bank(J_K + c)[:, 0:TC * M],
                                     ACT.Identity, bias=bk_c[:, 0:1]).then_inc(pre_act, 1)
            for c in range(BG):
                act.wait_ge(pre_mm, J_Q + c + 1)
                nc.scalar.activation(qT[:, CH * c:CH * (c + 1)], bank(J_Q + c),
                                     ACT.Identity, bias=bq_c[:, 0:1]).then_inc(pre_act, 1)

            def move_pt(b, q):
                act.wait_ge(pt_done, NQ * b + q + 1)
                act.wait_ge(pv_done, NQ * b + q + 1)
                nc.scalar.activation(probT[:, q, :], ps[0:M, TB + q % 2, :], ACT.Copy).then_inc(pt_moved, 1)

            def move_oT(b):
                act.wait_ge(oT_done, b + 1)
                nc.scalar.activation(oT_sb[:, :], OT, ACT.Copy).then_inc(oT_moved, 1)

            def attend(b, first=False):
                act.wait_ge(sub_done, b + 1)
                nc.scalar.activation(prob[:, :, :], prob[:, :, :], ACT.Exp, scale=SCALE).then_inc(exp_done, 1)
                move_pt(b, 0)
                move_pt(b, 1)
                if not first:
                    move_oT(b - 1)
                move_pt(b, 2)
                move_pt(b, 3)

            attend(0, first=True)
            with act.Fori(1, B) as b:
                attend(b)
            move_oT(B - 1)

            for c in range(NC):
                act.wait_ge(curT_done, c + 1)
                nc.scalar.activation(cur[:, CH * c:CH * (c + 1)], ps[:, 4 + c, :], ACT.Copy).then_inc(cur_ready, TC)

            def gelu(n, e, k):
                act.wait_ge(w1_done, n + 1)
                act.wait_ge(lo_done, n + 1)
                nc.scalar.activation(g_sb[:, k, :], ps[:, k, :], ACT.Gelu_apprx_tanh,
                                     bias=b1_c[:, e * NF + k:e * NF + k + 1]).then_inc(gelu_done, 1)

            def high(n, u, e, k):
                act.wait_ge(gelu_done, n + NF + 1)
                act.wait_ge(y_done, u + 1)
                nc.scalar.activation(h_hi[:, e % 2, k, :], g_sb[:, k, :], ACT.Copy).then_inc(hi_act, 1)

            def hidden(u, e, gate=None):
                n = u * NF
                gelu(n, e, 0)
                gelu(n + 1, e, 1)
                high(n + 1, u, e, 1)
                if gate is not None:
                    act.wait_ge(gate_step, GATE_OPS * (gate + 1))
                    nc.scalar.activation(th[:, :, :], half_d[:, :, :], ACT.Tanh).then_inc(th_done, 1)
                gelu(n + 2, e, 2)
                gelu(n + 3, e, 3)
                high(n + 3, u, e, 3)

            def move_cwb(u, e):
                act.wait_ge(cwb_done, u + 1)
                act.wait_ge(y_read, u + 1)
                nc.scalar.activation(cwb_sb[:, e % 2, :], CWB, ACT.Copy).then_inc(cwb_moved, 1)

            hidden(0, 0)
            with act.Fori(0, STEPS - 1) as i:
                for e in range(E):
                    u = i * E + e
                    hidden(u + 1, (e + 1) % E, gate=i if e == 0 else None)
                    move_cwb(u, e)
            for e in range(E):
                u = (STEPS - 1) * E + e
                if e < E - 1:
                    hidden(u + 1, e + 1, gate=STEPS - 1 if e == 0 else None)
                move_cwb(u, e)

        @block.vector
        def _(dve):
            dve.sem_inc(lo_done, NF)
            dve.sem_inc(y_read, 2)
            nc.vector.memset(vaug[:, :, :, DH:VW], 1.0).then_inc(ones_ready, 1)

            def aggregate():
                for b in range(B):
                    last = nc.vector.bn_aggr(mv[:, b, :], stats[:, b, :])
                    last.then_inc(mv_ready, 1)

            def normalise(src, n):
                dve.wait_ge(rstd_ready, n)
                for b in range(B):
                    nc.vector.tensor_scalar(xn[:, b, :], src[:, b, :], mv[:, b, 0:1], rstd[:, b:b + 1],
                                            ALU.subtract, ALU.mult).then_inc(xn_ready, 1)

            for b in range(B):
                if b % TC == 0:
                    dve.wait_ge(x_in[b // TC], 16)
                nc.vector.bn_stats(stats[:, b, :], x_sb[:, b, :]).then_inc(bn_step, 1)
            dve.wait_ge(bn_step, B)
            aggregate()
            dve.wait_ge(c_ready, 4)
            nc.vector.tensor_reduce(head_mask[:, :], head_at[:, :, :].rearrange("p q h -> p h q"), AX.X,
                                    ALU.add).then_inc(headmask_ready, 1)
            dve.wait_ge(small_ld, 16 * 3)
            normalise(x_sb, 1)
            for c in range(BG):
                dve.wait_ge(pre_mm, J_V + c + 1)
                nc.vector.tensor_tensor(
                    vaug[:, TC * c:TC * (c + 1), :, 0:DH],
                    bank(J_V + c)[0:M, :].rearrange("m (b h d) -> m b h d", b=TC, h=H),
                    bv_row[0:M, :].rearrange("m (h d) -> m h d", h=H).unsqueeze(1).to_broadcast([M, TC, H, DH]),
                    ALU.add).then_inc(pre_dve, 1)
            for c in range(BG):
                dve.wait_ge(pre_mm, J_XN + c + 1)
                nc.vector.tensor_copy(xnT[:, CH * c:CH * (c + 1)], bank(J_XN + c)).then_inc(pre_dve, 1)
            dve.wait_ge(moe_ld, 16 * 3)
            nc.vector.tensor_copy(wg_s[:, :, 0, :], wg_in[:, :, :]).then_inc(wg_split, 1)
            dve.wait_ge(wg_split, 1)
            nc.vector.tensor_tensor(wg_s[:, :, 1, :], wg_in[:, :, :], wg_s[:, :, 0, :].bitcast(F32),
                                    ALU.subtract).then_inc(wg_split, 1)

            def stage_q(b):
                dve.wait_ge(scores_done, b)
                qb = qT[:, bass.ds(b * L, L)]
                nc.vector.tensor_copy(q_hi[:, :], qb).then_inc(q_stage, 1)
                dve.wait_ge(q_stage, 2 * b + 1)
                nc.vector.tensor_tensor(q_lo[:, :], qb, q_hi[:, :].bitcast(F32), ALU.subtract).then_inc(q_stage, 1)

            s_all = ps[:, SC:SC + NQ, 0:HM].rearrange("p q (h m) -> p q h m", m=M)

            def softmax_shift(b):
                dve.wait_ge(scores_done, b + 1)
                nc.vector.tensor_reduce(mx[:, :].rearrange("p (q h) -> p q h", q=NQ), s_all, AX.X,
                                        ALU.max).then_inc(mx_done, 1)
                dve.wait_ge(mx_done, b + 1)
                dve.wait_ge(pt_done, NQ * b)
                nc.vector.tensor_tensor(
                    prob[:, :, :].rearrange("p q (h m) -> p q h m", m=M), s_all,
                    mx[:, :].rearrange("p (q h) -> p q h", q=NQ).unsqueeze(3).to_broadcast([P, NQ, HQ, M]),
                    ALU.subtract).then_inc(sub_done, 1)

            def finish(b):
                o = OB.rearrange("p (h v) -> p h v", v=VW)
                dve.wait_ge(pv_done, NQ * b + 2 * NQ)
                nc.vector.reciprocal(rden[:, :], o[:, :, DH]).then_inc(rden_done, 1)
                dve.wait_ge(rden_done, b + 1)
                nc.vector.tensor_tensor(o_n[:, :].rearrange("p (h d) -> p h d", h=H), o[:, :, 0:DH],
                                        rden[:, :].unsqueeze(2).to_broadcast([P, H, DH]),
                                        ALU.mult).then_inc(on_done, 1)
                dve.wait_ge(wo_done, b + 1)
                x1b = x1_sb[:, :, :].rearrange("p b d -> p (b d)")[:, bass.ds(b * D, D)]
                nc.vector.scalar_tensor_tensor(out=x1b, in0=AO, scalar=tgates[:, 0:1],
                                               in1=xres[:, :, :].rearrange("p b d -> p (b d)")[:, bass.ds(b * D, D)],
                                               op0=ALU.mult, op1=ALU.add).then_inc(x1_done, 1)

            moved(dve, JOBS - 1)
            dve.wait_ge(xres_step, 2)
            stage_q(0)
            stage_q(1)
            softmax_shift(0)
            with dve.Fori(1, B - 1) as b:
                stage_q(b + 1)
                softmax_shift(b)
                finish(b - 1)
            softmax_shift(B - 1)
            finish(B - 2)
            finish(B - 1)

            dve.wait_ge(x1_done, B)
            for b in range(B):
                nc.vector.bn_stats(stats[:, b, :], x1_sb[:, b, :]).then_inc(bn_step, 1)
            dve.wait_ge(bn_step, 2 * B)
            dve.wait_ge(xn_ready, B)
            aggregate()
            normalise(x1_sb, 2)

            def split_x(i):
                cc = cur[:, bass.ds((i % NC) * CH, CH)]
                dve.wait_ge(cur_ready, TC * i + TC)
                dve.wait_ge(w1_done, E * NF * i)
                nc.vector.tensor_copy(x_hi[:, :], cc).then_inc(x_hi_done, 1)
                dve.wait_ge(x_hi_done, i + 1)
                nc.vector.tensor_tensor(x_lo[:, :], cc, x_hi[:, :].bitcast(F32), ALU.subtract).then_inc(x_split, 1)

            def lo(n, e, k):
                nc.vector.tensor_tensor(h_lo[:, e % 2, k, :], g_sb[:, k, :],
                                        h_hi[:, e % 2, k, :].bitcast(F32), ALU.subtract).then_inc(lo_done, 1)

            def split_hidden(u, e, pair):
                k = 2 * pair
                n = u * NF + k
                dve.wait_ge(gelu_done, n + NF + 1)
                dve.wait_ge(y_done, u + 1)
                nc.vector.tensor_copy(h_hi[:, e % 2, k, :], g_sb[:, k, :]).then_inc(hi_dve, 1)
                dve.wait_ge(hi_dve, 2 * u + pair + 1)
                lo(n, e, k)
                dve.wait_ge(hi_act, 2 * u + pair + 1)
                lo(n + 1, e, k + 1)

            def share(u, e):
                dve.wait_ge(y_done, u + 3)
                dve.wait_ge(cwb_moved, u + 2)
                dve.wait_ge(cur_ready, B + u - 1)
                nc.vector.scalar_tensor_tensor(out=contrib[:, e % 2, :], in0=ps[:, YB + e % 2, :],
                                               scalar=b2_c[:, e:e + 1], in1=cwb_sb[:, e % 2, :],
                                               op0=ALU.add, op1=ALU.mult).then_inc(y_read, 1)

            def router(i):
                t = [GATE_OPS * i]

                def step(ins):
                    t[0] = t[0] + 1
                    ins.then_inc(gate_step, 1)

                def settle():
                    dve.wait_ge(gate_step, t[0])

                r = i // NC
                bgr = bg_row[:, bass.ds(r * E, E)].unsqueeze(1).to_broadcast([P, TC, E])
                lg_v = LG.rearrange("p (t n) -> p t n", t=TC)
                dve.wait_ge(logits_done, i + 1)
                step(nc.vector.tensor_tensor(lga[:, :, :], lg_v[:, :, bass.ds(r * (2 * E), E)], bgr, ALU.add))
                settle()
                step(nc.vector.tensor_tensor(lg[:, :, :], lg_v[:, :, bass.ds(r * (2 * E) + E, E)],
                                             lga[:, :, :], ALU.add))
                settle()
                other = lg[:, :, :].unsqueeze(2).to_broadcast([P, TC, E, E])
                mine = lg[:, :, :].unsqueeze(3).to_broadcast([P, TC, E, E])
                step(nc.vector.tensor_tensor(beat_ge[:, :, :, :], other, mine, ALU.is_ge))
                step(nc.vector.tensor_tensor(beat_gt[:, :, :, :], other, mine, ALU.is_gt))
                settle()
                step(nc.vector.tensor_tensor(beat_ge[:, :, :, :], beat_ge[:, :, :, :],
                                             before[:, :, :].unsqueeze(1).to_broadcast([P, TC, E, E]), ALU.mult))
                step(nc.vector.tensor_tensor(beat_gt[:, :, :, :], beat_gt[:, :, :, :],
                                             after[:, :, :].unsqueeze(1).to_broadcast([P, TC, E, E]), ALU.mult))
                settle()
                step(nc.vector.tensor_tensor(beat_ge[:, :, :, :], beat_ge[:, :, :, :], beat_gt[:, :, :, :], ALU.add))
                settle()
                step(nc.vector.tensor_reduce(rank[:, :, :], beat_ge[:, :, :, :], AX.X, ALU.add))
                settle()
                dve.wait_ge(cwb_moved, E * i + 1)
                step(nc.vector.scalar_tensor_tensor(out=sel_lg[:, :, :], in0=rank[:, :, :], scalar=2.0,
                                                    in1=lg[:, :, :], op0=ALU.is_lt, op1=ALU.mult))
                settle()
                step(nc.vector.tensor_reduce(sel_sum[:, :], sel_lg[:, :, :], AX.X, ALU.add))
                settle()
                step(nc.vector.scalar_tensor_tensor(out=half_d[:, :, :],
                                                    in0=sel_sum[:, :].unsqueeze(2).to_broadcast([P, TC, E]),
                                                    scalar=-0.5, in1=lg[:, :, :], op0=ALU.mult, op1=ALU.add))
                dve.wait_ge(th_done, i + 1)
                nc.vector.tensor_scalar(wgt[:, :, :], th[:, :, :], 0.5, 0.5, ALU.mult,
                                        ALU.add).then_inc(wgt_done, 1)
                dve.wait_ge(wgt_done, i + 1)
                nc.vector.scalar_tensor_tensor(out=cw[:, :, :], in0=rank[:, :, :], scalar=2.0,
                                               in1=wgt[:, :, :], op0=ALU.is_lt, op1=ALU.mult).then_inc(cw_ready, 1)

            def unit(i, e, last=False):
                u = i * E + e
                if e == 0:
                    router(i)
                if not (last and e == E - 1):
                    split_hidden(u + 1, (e + 1) % E, 0)
                    if e == E - 2 and not last:
                        split_x(i + 1)
                    split_hidden(u + 1, (e + 1) % E, 1)
                share(u, e)

            split_x(0)
            split_hidden(0, 0, 0)
            split_hidden(0, 0, 1)
            with dve.Fori(0, STEPS - 1) as i:
                for e in range(E):
                    unit(i, e)
            for e in range(E):
                unit(STEPS - 1, e, last=True)

            for c in range(NC):
                dve.wait_ge(fin_mm, c + 1)
                nc.vector.scalar_tensor_tensor(
                    out=out_sb[:, TC * c:TC * (c + 1), :], in0=ps[:, c, :].rearrange("p (b d) -> p b d", b=TC),
                    scalar=tgates[:, 1:2], in1=x1_sb[:, TC * c:TC * (c + 1), :],
                    op0=ALU.mult, op1=ALU.add).then_inc(fin_done, 1)

        @block.tensor
        def _(pe):
            pe.sem_inc(pv_done, NQ)
            pe.sem_inc(y_done, 2)
            mm = nc.tensor.matmul
            tr = nc.tensor.transpose
            pe.wait_ge(c_ready, 1)
            pe.wait_ge(wproj_ld, 16 * 4)
            tr(bank(J_W)[:, 0:P], wq_in[:, :], ident[:, :])
            tr(bank(J_W)[0:C, P:2 * P], wk_in[:, :], ident[:, :])
            tr(bank(J_W)[0:C, 2 * P:3 * P], wv_in[:, :], ident[:, :])
            tr(bank(J_W)[:, 3 * P:4 * P], wo_in[:, :], ident[:, :]).then_inc(pre_mm, 1)
            pe.wait_ge(rows_ld, 16 * 4)
            tr(COLS, rows_in[:, :], ident[0:NCOL, 0:NCOL])
            pe.wait_ge(ctx_ld, 16)
            for b in range(B):
                j = J_CTX + b // TC
                t = tr(bank(j)[0:C, (b % TC) * M:(b % TC + 1) * M], ctx_sb[:, b, :], ident[0:M, 0:M])
                if b % TC == TC - 1:
                    t.then_inc(pre_mm, 1)
            moved(pe, J_W)
            for c in range(BG):
                moved(pe, J_CTX + c)
                if J_K + c >= 8:
                    moved(pe, J_K + c - 8)
                mm(bank(J_K + c)[:, 0:TC * M], wT[0:C, 1, :], ctxT[:, TC * M * c:TC * M * (c + 1)],
                   start=True, stop=True).then_inc(pre_mm, 1)
            for b in range(B):
                j = J_V + b // TC
                if b % TC == 0:
                    moved(pe, j - 8)
                t = mm(bank(j)[0:M, (b % TC) * D:(b % TC + 1) * D], ctxT[:, b * M:(b + 1) * M], wT[0:C, 2, :],
                       start=True, stop=True)
                if b % TC == TC - 1:
                    t.then_inc(pre_mm, 1)
            for b in range(B):
                j = J_XN + b // TC
                if b % TC == 0:
                    moved(pe, j - 8)
                pe.wait_ge(xn_ready, b + 1)
                t = tr(bank(j)[:, (b % TC) * L:(b % TC + 1) * L], xn[:, b, :], ident[:, :])
                if b % TC == TC - 1:
                    t.then_inc(pre_mm, 1)
            for c in range(BG):
                j = J_Q + c
                moved(pe, j - 8)
                moved(pe, J_XN + c)
                mm(bank(j), wT[:, 0, :], xnT[:, CH * c:CH * (c + 1)], start=True, stop=True).then_inc(pre_mm, 1)

            def scores(b):
                pe.wait_ge(q_stage, 2 * b + 2)
                pe.wait_ge(k_stage, 3 * b + 3)
                pe.wait_ge(sub_done, b)
                passes = ((q_hi, k_hi), (q_hi, k_lo), (q_lo, k_hi))
                for n, (qs, ks) in enumerate(passes):
                    for q in range(NQ):
                        rows = slice(32 * q, 32 * q + 32)
                        t = mm(ps[:, SC + q, 0:HM], qs[rows, :], ks[rows, :],
                               start=n == 0, stop=n == len(passes) - 1)
                t.then_inc(scores_done, 1)

            def transpose_probs(b, q):
                pe.wait_ge(exp_done, b + 1)
                pe.wait_ge(pt_moved, NQ * b + q + 1)
                for h in range(HQ):
                    t = tr(ps[0:M, TB + q % 2, h * L:(h + 1) * L], prob[:, q, h * M:(h + 1) * M], ident[:, :])
                t.then_inc(pt_done, 1)

            def weigh_values(b, q):
                pe.wait_ge(pt_moved, NQ * b + q + 3)
                if q == 0:
                    pe.wait_ge(v_stage, b + 1)
                    pe.wait_ge(on_done, b)
                for h in range(HQ):
                    c = (q * HQ + h) * VW
                    t = mm(OB[:, c:c + VW], probT[:, q, h * L:(h + 1) * L], v_st[:, c:c + VW],
                           start=True, stop=True)
                t.then_inc(pv_done, 1)

            def transpose_o(b):
                pe.wait_ge(on_done, b + 1)
                tr(OT, o_n[:, :], ident[:, :]).then_inc(oT_done, 1)

            def project_o(b):
                pe.wait_ge(oT_moved, b + 1)
                mm(AO, oT_sb[:, :], wT[:, 3, :], start=True, stop=True).then_inc(wo_done, 1)

            def attend(b, first=False, last=False):
                if not last:
                    scores(b + 1)
                transpose_probs(b, 0)
                transpose_probs(b, 1)
                if not first:
                    transpose_o(b - 1)
                weigh_values(b, 0)
                transpose_probs(b, 2)
                if not first:
                    project_o(b - 1)
                weigh_values(b, 1)
                transpose_probs(b, 3)
                weigh_values(b, 2)
                weigh_values(b, 3)

            moved(pe, JOBS - 1)
            scores(0)
            attend(0, first=True)
            with pe.Fori(1, B - 1) as b:
                attend(b)
            attend(B - 1, last=True)
            transpose_o(B - 1)
            project_o(B - 1)

            pe.wait_ge(x1_done, B)
            for b in range(B):
                pe.wait_ge(xn_ready, B + b + 1)
                t = tr(ps[:, 4 + b // TC, (b % TC) * L:(b % TC + 1) * L], xn[:, b, :], ident[:, :])
                if b % TC == TC - 1:
                    t.then_inc(curT_done, 1)

            def logits(i):
                pe.wait_ge(x_split, i + 1)
                pe.wait_ge(gate_step, GATE_OPS * i)
                for t in range(TC):
                    o = LG[:, t * LG_N:(t + 1) * LG_N]
                    wg = wg_s[:, :, :, :].rearrange("p r s e -> p (r s e)")
                    mm(o, x_hi[:, t * P:(t + 1) * P], wg, start=True, stop=False)
                    m = mm(o, x_lo[:, t * P:(t + 1) * P], wg, start=False, stop=True)
                m.then_inc(logits_done, 1)

            def up(u, e):
                for k in range(NF):
                    n = u * NF + k
                    w = slice(e * F + k * P, e * F + (k + 1) * P)
                    pe.wait_ge(gelu_done, n + 1)
                    mm(ps[:, k, :], w1_hi[:, w], x_hi[:, :], start=True, stop=False)
                    mm(ps[:, k, :], w1_hi[:, w], x_lo[:, :], start=False, stop=False)
                    mm(ps[:, k, :], w1_lo[:, w], x_hi[:, :], start=False, stop=True).then_inc(w1_done, 1)

            def spread(u, i, e):
                if e == 0:
                    pe.wait_ge(cw_ready, i + 1)
                pe.wait_ge(cwb_moved, u + 1)
                for t in range(TC):
                    m = tr(CWB[:, t * P:(t + 1) * P], cw[:, t, e:e + 1].to_broadcast([P, P]), ident[:, :])
                m.then_inc(cwb_done, 1)

            def down(u, e):
                pe.wait_ge(y_read, u + 1)
                yb = ps[:, YB + e % 2, :]
                for k in range(NF):
                    w = slice((e * NF + k) * D, (e * NF + k + 1) * D)
                    pe.wait_ge(lo_done, u * NF + k + NF + 1)
                    hh, hl = h_hi[:, e % 2, k, :], h_lo[:, e % 2, k, :]
                    mm(yb, w2_hi[:, w], hh, start=k == 0, stop=False)
                    mm(yb, w2_hi[:, w], hl, start=False, stop=False)
                    m = mm(yb, w2_lo[:, w], hh, start=False, stop=k == NF - 1)
                m.then_inc(y_done, 1)

            pe.wait_ge(cur_ready, B)
            pe.wait_ge(wg_split, 2)
            pe.wait_ge(w_split, 4 * B)
            logits(0)
            up(0, 0)
            with pe.Fori(0, STEPS - 1) as i:
                for e in range(E):
                    u = i * E + e
                    if e == E - 1:
                        logits(i + 1)
                    up(u + 1, (e + 1) % E)
                    spread(u, i, e)
                    down(u, e)
            for e in range(E):
                u = (STEPS - 1) * E + e
                if e < E - 1:
                    up(u + 1, e + 1)
                spread(u, STEPS - 1, e)
                down(u, e)

            for c in range(NC):
                pe.wait_ge(cur_ready, B + E * (STEPS - NC + c + 1))
                for t in range(TC):
                    b = c * TC + t
                    m = tr(ps[:, c, t * P:(t + 1) * P], cur[:, b * P:(b + 1) * P], ident[:, :])
                m.then_inc(fin_mm, 1)


_INS = ["x", "ctx_768", "g_xattn", "g_ffn", "L0_xattn_Wq", "L0_xattn_bq", "L0_xattn_Wkv", "L0_xattn_bkv",
        "L0_xattn_Wo", "L0_xattn_bo", "L0_ffn_Wg", "L0_ffn_bg", "L0_ffn_W1", "L0_ffn_b1", "L0_ffn_W2", "L0_ffn_b2"]


def kernel(**inputs):
    import numpy as _np
    import concourse.bacc as _bacc
    from concourse import mybir as _mybir
    from concourse.bass_utils import run_bass_kernel_spmd as _run

    nc = _bacc.Bacc("TRN2", target_bir_lowering=False, num_devices=1)
    arrays, args = {}, []
    for name in _INS:
        a = _np.ascontiguousarray(inputs[name])
        arrays[f"in_{name}_dram"] = a
        args.append(nc.dram_tensor(f"in_{name}_dram", a.shape, _mybir.dt.from_np(a.dtype), kind="ExternalInput").ap())
    x = inputs["x"]
    args.append(nc.dram_tensor("out_0_dram", x.shape, _mybir.dt.float32, kind="ExternalOutput").ap())
    flamingo_gated_block(nc, *args)
    r = _run(nc, [arrays], core_ids=[0])
    return r.results[0]["out_0_dram"]
```

```python
from contextlib import ExitStack

import concourse.bass as bass
from concourse import mybir

P = 128
F32 = mybir.dt.float32
F32R = mybir.dt.float32r
BF16 = mybir.dt.bfloat16
ALU = mybir.AluOpType
ACT = mybir.ActivationFunctionType
AX = mybir.AxisListType
EPS = 1e-5


def flamingo_gated_block(
    nc: bass.Bass,
    x: bass.AP,
    ctx_in: bass.AP,
    g_xattn: bass.AP,
    g_ffn: bass.AP,
    Wq: bass.AP,
    bq: bass.AP,
    Wkv: bass.AP,
    bkv: bass.AP,
    Wo: bass.AP,
    bo: bass.AP,
    Wg: bass.AP,
    bg: bass.AP,
    W1: bass.AP,
    b1: bass.AP,
    W2: bass.AP,
    b2: bass.AP,
    out: bass.AP,
):
    B, L, D = x.shape
    M, C = ctx_in.shape[1:]
    ROUNDS, _, E = Wg.shape
    F = W1.shape[2]
    H = 16
    DH = D // H
    SCALE = float(DH) ** -0.5
    HQ = 32 // DH
    NQ = P // 32
    PT = -(-H * M // P)
    HS = 4
    H2 = 2 * P // M
    N = B * L
    CH = 512
    NC = N // CH
    TC = CH // P
    NF = F // P
    BG = B // TC
    STEPS = ROUNDS * NC
    HM = HQ * M
    CP = 3
    GATE_OPS = 11
    assert L == P and D == P and H == HQ * NQ and N % CH == 0 and F == NF * P and B % TC == 0
    tiles = [min(P, H * M - P * c) for c in range(PT)]
    head0 = [H2 * (c // 2) + c % 2 for c in range(PT)]
    heads = [min(HS, H - h) for h in head0]
    assert PT % 2 == 0 and all(h <= P * c // M and (P * c + n - 1) // M < h + k
                               for c, (n, h, k) in enumerate(zip(tiles, head0, heads)))
    VS = 2 * P + H2 * DH
    TG = [(0, 4), (4, 8), (8, PT)]
    PVS = [(0, 0), (0, 5), (5, 8), (8, PT)]
    assert M <= P and C <= P and TC * M <= CH and F == CH and NF == 4 and STEPS == B

    with ExitStack() as stack:
        def sb(name, shape, dt=F32):
            return stack.enter_context(nc.sbuf_tensor(name, shape, dt))

        def sem(name):
            return stack.enter_context(nc.semaphore(name))

        ps = stack.enter_context(nc.psum_tensor("ps", [P, 8, CH], F32))

        ident = sb("ident", [P, P])
        head_at = sb("head_at", [P, NQ, HQ])
        head_mask = sb("head_mask", [P, HQ])
        before = sb("before", [P, E, E])
        after = sb("after", [P, E, E])
        minus_half = sb("minus_half", [P, B])
        gates = sb("gates", [P, 2])
        tgates = sb("tgates", [P, 2])
        NCOL = E * NF + E + 2
        rows_in = sb("rows_in", [NCOL, P])
        cols = sb("cols", [P, NCOL])
        b1_c = cols[:, 0:E * NF]
        b2_c = cols[:, E * NF:E * NF + E]
        bq_c = cols[:, NCOL - 2:NCOL - 1]
        bk_c = cols[:, NCOL - 1:NCOL]
        bv_row = sb("bv_row", [P, D])
        bo_row = sb("bo_row", [P, D])
        bg_row = sb("bg_row", [P, ROUNDS * E])
        wq_in = sb("wq_in", [P, D])
        wk_in = sb("wk_in", [P, C])
        wv_in = sb("wv_in", [P, C])
        wo_in = sb("wo_in", [P, D])
        wT = sb("wT", [P, 4, P])
        wg_in = sb("wg_in", [P, ROUNDS, E])
        wg_s = sb("wg_s", [P, ROUNDS, 2, E], F32R)
        w1_in = sb("w1_in", [P, E * F])
        w2_in = sb("w2_in", [P, E * NF * D])
        w1_hi = sb("w1_hi", [P, E * F], F32R)
        w1_lo = sb("w1_lo", [P, E * F], F32R)
        w2_hi = sb("w2_hi", [P, E * NF * D], F32R)
        w2_lo = sb("w2_lo", [P, E * NF * D], F32R)
        x_sb = sb("x_sb", [P, B, D])
        xres = sb("xres", [P, B, D])
        x1_sb = x_sb
        stats = sb("stats", [P, B, 6])
        mv = sb("mv", [P, B, 2])
        veps = sb("veps", [P, B])
        rstd = sb("rstd", [P, B])
        xn = sb("xn", [P, B, D])
        qT = sb("qT", [P, N])
        kT = sb("kT", [P, B * M])
        q_hi = sb("q_hi", [P, 2, NQ, L], F32R)
        q_lo = sb("q_lo", [P, 2, NQ, L], F32R)
        k_f = sb("k_f", [P, HQ, M])
        k_hi = sb("k_hi", [P, 2, HQ * M], F32R)
        k_lo = sb("k_lo", [P, 2, HQ * M], F32R)
        row_head = sb("row_head", [P, PT, H])
        v_st = sb("v_st", [P, 2, (PT + 2) * P])
        shifted = sb("shifted", [P, NQ, HM])
        prob = sb("prob", [P, H * M])
        probT = sb("probT", [P, PT, L])
        mx = sb("mx", [P, H])
        den = sb("den", [P, H])
        rden = sb("rden", [P, H])
        rden_w = bv_row
        rT_sb = sb("rT_sb", [P, L])
        oT_sb = sb("oT_sb", [P, L])
        cur = sb("cur", [P, N])
        xnT = cur
        out_sb = xn
        attention = ExitStack()

        def early(name, shape, dt=F32):
            return attention.enter_context(nc.sbuf_tensor(name, shape, dt))

        pick_f = early("pick_f", [M, H + 1, M])
        pick = early("pick", [M, (H + 1) * M], F32R)
        v_sb = early("v_sb", [M, B, H, DH])
        v_hi = early("v_hi", [M, B, H, DH], F32R)
        v_lo = early("v_lo", [M, B, H, DH], F32R)
        v_blk = early("v_blk", [P, PT, B, HS * DH])
        ctx_sb = early("ctx_sb", [M, B, C])
        ctxT = early("ctxT", [C, B * M])
        attention.close()
        lga = sb("lga", [P, TC, E])
        lg = sb("lg", [P, TC, E])
        beat_ge = sb("beat_ge", [P, TC, E, E])
        beat_gt = sb("beat_gt", [P, TC, E, E])
        rank = sb("rank", [P, TC, E])
        sel_lg = sb("sel_lg", [P, TC, E])
        sel_sum = sb("sel_sum", [P, TC])
        half_d = sb("half_d", [P, TC, E])
        th = sb("th", [P, TC, E])
        wgt = sb("wgt", [P, TC, E])
        cw = sb("cw", [P, TC, E])
        cw_rest = sb("cw_rest", [P, TC, E])
        cw_parts = sb("cw_parts", [P, TC, CP, E], BF16)
        cwT = sb("cwT", [CP * E, CH], BF16)
        spread_f = sb("spread_f", [CP * E, E, P])
        spread_by = sb("spread_by", [CP * E, E, P], BF16)
        ident_b = sb("ident_b", [P, P], BF16)
        contrib = sb("contrib", [P, 2, CH])
        cwb_sb = sb("cwb_sb", [P, 2, CH])
        x_lo = sb("x_lo", [P, CH], F32R)
        x_hi = sb("x_hi", [P, CH], F32R)
        g_sb = sb("g_sb", [P, NF, CH])
        h_hi = sb("h_hi", [P, 2, NF, CH], F32R)
        h_lo = sb("h_lo", [P, 2, NF, CH], F32R)

        x_in = [sem(f"x_in{c}") for c in range(BG)]
        ctx_ld = sem("ctx_ld")
        wproj_ld = sem("wproj_ld")
        bv_ld = sem("bv_ld")
        small_ld = sem("small_ld")
        rows_ld = sem("rows_ld")
        gates_ld = sem("gates_ld")
        moe_ld = sem("moe_ld")
        out_st = sem("out_st")
        c_zero = sem("c_zero")
        c_mask = sem("c_mask")
        c_ready = sem("c_ready")
        cols_ready = sem("cols_ready")
        headmask_ready = sem("headmask_ready")
        tg_ready = sem("tg_ready")
        fill_done = sem("fill_done")
        bn_step = sem("bn_step")
        mv_ready = sem("mv_ready")
        veps_ready = sem("veps_ready")
        rstd_ready = sem("rstd_ready")
        xn_ready = sem("xn_ready")
        xres_step = sem("xres_step")
        pre_mm = sem("pre_mm")
        pre_act = sem("pre_act")
        pre_dve = sem("pre_dve")
        k_stage = sem("k_stage")
        v_stage = sem("v_stage")
        v_split = sem("v_split")
        pick_ready = sem("pick_ready")
        w_hi = sem("w_hi")
        q_zero = sem("q_zero")
        q_hi_done = sem("q_hi_done")
        q_lo_done = sem("q_lo_done")
        w_split = sem("w_split")
        scores_done = sem("scores_done")
        mx_done = sem("mx_done")
        sub_done = sem("sub_done")
        exp_done = sem("exp_done")
        pt_done = sem("pt_done")
        pt_moved = sem("pt_moved")
        pv_done = sem("pv_done")
        den_done = sem("den_done")
        rden_done = sem("rden_done")
        rw_done = sem("rw_done")
        rT_done = sem("rT_done")
        rT_moved = sem("rT_moved")
        oT_ready = sem("oT_ready")
        wo_done = sem("wo_done")
        x1_done = sem("x1_done")
        st_done = sem("st_done")
        curT_done = sem("curT_done")
        cur_ready = sem("cur_ready")
        wg_split = sem("wg_split")
        x_hi_done = sem("x_hi_done")
        x_split = sem("x_split")
        logits_done = sem("logits_done")
        gate_step = sem("gate_step")
        th_done = sem("th_done")
        wgt_done = sem("wgt_done")
        cw_ready = sem("cw_ready")
        w1_done = sem("w1_done")
        gelu_done = sem("gelu_done")
        hi_act = sem("hi_act")
        hi_dve = sem("hi_dve")
        lo_done = sem("lo_done")
        y_done = sem("y_done")
        y_read = sem("y_read")
        spread_step = sem("spread_step")
        spread_ready = sem("spread_ready")
        cw_step = sem("cw_step")
        cwT_done = sem("cwT_done")
        cwT_moved = sem("cwT_moved")
        cwb_done = sem("cwb_done")
        cwb_moved = sem("cwb_moved")
        fin_mm = sem("fin_mm")
        fin_done = sem("fin_done")

        SC = 0
        TB = 4
        OT = ps[:, 6, 0:L]
        RT = ps[:, 7, 0:L]
        AO = ps[:, 7, L:L + D]
        CURT = (4, 5, 6, 4)
        YB = 4
        CWB = ps[:, 6, :]
        LG = ps[:, 7, 0:TC * ROUNDS * 2 * E]
        LG_N = ROUNDS * 2 * E

        WS = E * F // B

        J_W, J_CTX, J_V, J_XN = 0, 1, 1 + BG, 1 + 2 * BG
        J_K, J_Q = 1 + 3 * BG, 1 + 4 * BG
        J_VF = 1 + 5 * BG
        JOBS = J_VF + PT
        on_dve = [J_V <= j < J_XN or J_VF <= j for j in range(JOBS)]
        SC_FREE = max(j for j in range(JOBS) if j % 8 < NQ)
        NG = len(TG)

        def moved(eng, j):
            n = sum(d == on_dve[j] for d in on_dve[:j + 1])
            eng.wait_ge(pre_dve if on_dve[j] else pre_act, n)

        def slot(c):
            return c % 2 * (PT // 2) + c // 2

        def bank(j):
            return ps[:, j % 8, :]

        COLS = bank(J_CTX)[:, TC * M:TC * M + NCOL]

        x_v = x.rearrange("b l d -> l b d")
        out_v = out.rearrange("b l d -> l b d")
        kv_v = Wkv.rearrange("(h t d) c -> t h d c", h=H, t=2)
        bkv_v = bkv.rearrange("(h t d) -> t h d", h=H, t=2)

        block = stack.enter_context(nc.Block())

        @block.sync
        def _(sp):
            sp.dma_start(wq_in[:, :], Wq).then_inc(wproj_ld, 16)
            sp.dma_start(wk_in[:, :], kv_v[0].rearrange("h d c -> h d c")).then_inc(wproj_ld, 16)
            sp.dma_start(wv_in[:, :], kv_v[1].rearrange("h d c -> h d c")).then_inc(wproj_ld, 16)
            sp.dma_start(wo_in[:, :], Wo).then_inc(wproj_ld, 16)
            for c in range(BG):
                sp.dma_start(x_sb[:, TC * c:TC * c + TC, :],
                             x_v[:, TC * c:TC * c + TC, :]).then_inc(x_in[c], 16)
            sp.dma_start(gates[:, 0:1], g_xattn.rearrange("(o a) -> o a", o=1).to_broadcast([P, 1])).then_inc(gates_ld, 16)
            sp.dma_start(gates[:, 1:2], g_ffn.rearrange("(o a) -> o a", o=1).to_broadcast([P, 1])).then_inc(gates_ld, 16)
            sp.dma_start(bo_row[:, :], bo.unsqueeze(0).to_broadcast([P, D])).then_inc(small_ld, 16)
            sp.dma_start(bg_row[:, :], bg.rearrange("r e -> (r e)").unsqueeze(0)
                          .to_broadcast([P, ROUNDS * E])).then_inc(small_ld, 16)
            sp.dma_start(wg_in[:, :, :], Wg.rearrange("r h e -> h r e")).then_inc(moe_ld, 16)
            sp.dma_start(w1_in[:, :].rearrange("h (e f) -> h e f", e=E),
                         W1.rearrange("e h f -> h e f")).then_inc(moe_ld, 16)
            sp.dma_start(w2_in[:, :].rearrange("p (e k h) -> p e k h", e=E, k=NF),
                         W2.rearrange("e (k p) h -> p e k h", p=P)).then_inc(moe_ld, 16)
            for c in range(NC):
                sp.wait_ge(fin_done, c + 1)
                sp.dma_start(out_v[:, TC * c:TC * c + TC, :],
                             out_sb[:, TC * c:TC * c + TC, :]).then_inc(out_st, 16)
            sp.wait_ge(out_st, 16 * NC)

        @block.gpsimd
        def _(pool):
            nc.gpsimd.memset(ident[:, :], 0.0).then_inc(c_zero, 1)
            nc.gpsimd.memset(head_at[:, :, :], 1.0).then_inc(c_zero, 1)
            nc.gpsimd.memset(before[:, :, :], 1.0).then_inc(c_zero, 1)
            nc.gpsimd.memset(after[:, :, :], 1.0).then_inc(c_zero, 1)
            nc.gpsimd.memset(minus_half[:, :], -0.5).then_inc(c_zero, 1)
            nc.gpsimd.memset(pick_f[:, :, :], 0.0).then_inc(c_zero, 1)
            nc.gpsimd.memset(row_head[:, :, :], 1.0).then_inc(c_zero, 1)
            pool.wait_ge(c_zero, 7)
            nc.gpsimd.affine_select(out=ident[:, :], in_=ident[:, :], compare_op=ALU.not_equal, fill=1.0,
                                    base=0, pattern=[[-1, P]], channel_multiplier=1).then_inc(c_ready, 1)
            nc.gpsimd.affine_select(out=head_at[:, :, :], in_=head_at[:, :, :], compare_op=ALU.is_ge, fill=0.0,
                                    base=0, pattern=[[-32, NQ], [-DH, HQ]],
                                    channel_multiplier=1).then_inc(c_mask, 1)
            pool.wait_ge(c_mask, 1)
            nc.gpsimd.affine_select(out=head_at[:, :, :], in_=head_at[:, :, :], compare_op=ALU.is_ge, fill=0.0,
                                    base=DH - 1, pattern=[[32, NQ], [DH, HQ]],
                                    channel_multiplier=-1).then_inc(c_ready, 1)
            nc.gpsimd.affine_select(out=before[:, :, :], in_=before[:, :, :], compare_op=ALU.is_ge, fill=0.0,
                                    base=-1, pattern=[[1, E], [-1, E]], channel_multiplier=0).then_inc(c_ready, 1)
            nc.gpsimd.affine_select(out=after[:, :, :], in_=after[:, :, :], compare_op=ALU.is_ge, fill=0.0,
                                    base=-1, pattern=[[-1, E], [1, E]], channel_multiplier=0).then_inc(c_ready, 1)

            nc.gpsimd.affine_select(out=pick_f[:, :, :], in_=pick_f[:, :, :], compare_op=ALU.not_equal, fill=1.0,
                                    base=0, pattern=[[0, H + 1], [1, M]], channel_multiplier=-1).then_inc(c_ready, 1)
            nc.gpsimd.affine_select(out=row_head[:, :, :], in_=row_head[:, :, :], compare_op=ALU.is_ge, fill=0.0,
                                    base=0, pattern=[[P, PT], [-M, H]], channel_multiplier=1).then_inc(c_mask, 1)
            pool.wait_ge(c_mask, 2)
            nc.gpsimd.affine_select(out=row_head[:, :, :], in_=row_head[:, :, :], compare_op=ALU.is_ge, fill=0.0,
                                    base=M - 1, pattern=[[-P, PT], [M, H]], channel_multiplier=-1).then_inc(c_ready, 1)

            def rstd_of(norm, c):
                n, tt = norm * NC + c + 1, slice(TC * c, TC * (c + 1))
                pool.wait_ge(mv_ready, TC * n)
                nc.gpsimd.tensor_scalar(veps[:, tt], mv[:, tt, 1], EPS, None, ALU.add).then_inc(veps_ready, 1)
                pool.wait_ge(veps_ready, n)
                nc.gpsimd.tensor_tensor(rstd[:, tt], veps[:, tt], minus_half[:, tt], ALU.pow).then_inc(rstd_ready, 1)

            for c in range(NC):
                rstd_of(0, c)
            headm = head_mask[:, :].unsqueeze(2).to_broadcast([P, HQ, M])

            def stage_k(b, s, first=False):
                if not first:
                    pool.wait_ge(scores_done, 2 * b - 2)
                pool.wait_ge(k_stage, 3 * b)
                kb = kT[:, bass.ds(b * M, M)].unsqueeze(1).to_broadcast([P, HQ, M])
                nc.gpsimd.tensor_tensor(k_f[:, :, :], kb, headm, ALU.mult).then_inc(k_stage, 1)
                nc.gpsimd.tensor_tensor(k_hi[:, s, :].rearrange("p (h m) -> p h m", m=M), kb, headm,
                                        ALU.mult).then_inc(k_stage, 1)
                pool.wait_ge(k_stage, 3 * b + 2)
                nc.gpsimd.tensor_tensor(k_lo[:, s, :], k_f[:, :, :].rearrange("p h m -> p (h m)"), k_hi[:, s, :].bitcast(F32),
                                        ALU.subtract).then_inc(k_stage, 1)

            def stage_v(b, s):
                pool.wait_ge(pv_done, NG * b)
                for odd in range(2):
                    at = odd * (P + DH)
                    nc.gpsimd.tensor_copy(
                        v_st[:, s, at:at + PT // 2 * VS].rearrange("p (c w) -> p c w", w=VS)[:, :, 0:HS * DH],
                        v_blk[:, odd * (PT // 2):(odd + 1) * (PT // 2), bass.ds(b, 1), :]
                        .rearrange("p c b v -> p c (b v)")).then_inc(v_stage, 1)

            def split_w(b):
                s = bass.ds(b * WS, WS)
                pool.wait_ge(w_hi, 2 * b + 2)
                nc.gpsimd.tensor_tensor(w1_lo[:, s], w1_in[:, s], w1_hi[:, s].bitcast(F32),
                                        ALU.subtract).then_inc(w_split, 1)
                nc.gpsimd.tensor_tensor(w2_lo[:, s], w2_in[:, s], w2_hi[:, s].bitcast(F32),
                                        ALU.subtract).then_inc(w_split, 1)

            pool.wait_ge(headmask_ready, 1)
            moved(pool, J_K + BG - 1)
            stage_k(0, 0, first=True)
            stage_k(1, 1, first=True)
            pool.wait_ge(tg_ready, 1)
            pool.wait_ge(small_ld, 16 * 2)
            nc.gpsimd.tensor_scalar(bo_row[:, :], bo_row[:, :], tgates[:, 0:1], None,
                                    ALU.mult).then_inc(xres_step, 1)
            pool.wait_ge(xres_step, 1)
            for c in range(BG):
                pool.wait_ge(x_in[c], 16)
            nc.gpsimd.tensor_tensor(xres[:, :, :], x_sb[:, :, :],
                                    bo_row[:, :].unsqueeze(1).to_broadcast([P, B, D]),
                                    ALU.add).then_inc(xres_step, 1)
            pool.wait_ge(moe_ld, 16 * 3)
            moved(pool, JOBS - 1)
            pool.wait_ge(fill_done, 2)

            def stage(b, s, last=False):
                stage_v(b, s)
                split_w(b)
                if not last:
                    stage_k(b + 2, s)

            stage(0, 0)
            stage(1, 1)
            with pool.Fori(1, B // 2 - 1) as j:
                stage(2 * j, 0)
                stage(2 * j + 1, 1)
            stage(B - 2, 0, last=True)
            stage(B - 1, 1, last=True)

            for c in range(NC):
                rstd_of(1, c)

            nc.gpsimd.memset(spread_f[:, :, :], 0.0).then_inc(spread_step, 1)
            for m in range(CP):
                pool.wait_ge(spread_step, m + 1)
                nc.gpsimd.affine_select(out=spread_f[:, :, :], in_=spread_f[:, :, :], compare_op=ALU.not_equal,
                                        fill=1.0, base=-m * E, pattern=[[-1, E], [0, P]],
                                        channel_multiplier=1).then_inc(spread_step, 1)
            pool.wait_ge(spread_step, CP + 1)
            nc.gpsimd.tensor_copy(spread_by[:, :, :], spread_f[:, :, :]).then_inc(spread_ready, 1)
            nc.gpsimd.tensor_copy(ident_b[:, :], ident[:, :]).then_inc(spread_ready, 1)

            UNITS = STEPS * E

            share_v = contrib[:, :, :].rearrange("p s n -> p (s n)")
            with pool.Fori(0, UNITS) as u:
                pool.wait_ge(y_read, u + 3)
                pool.wait_ge(cur_ready, u + B)
                cc = cur[:, bass.ds(((u // E) % NC) * CH, CH)]
                nc.gpsimd.tensor_tensor(cc, cc, share_v[:, bass.ds((u % 2) * CH, CH)],
                                        ALU.add).then_inc(cur_ready, 1)

        @block.scalar
        def _(act):
            act.dma_start(ctx_sb[:, :, :], ctx_in.rearrange("b m c -> m b c")).then_inc(ctx_ld, 16)
            act.dma_start(bv_row[:, :].rearrange("p (h d) -> p h d", h=H),
                          bkv_v[1].unsqueeze(0).to_broadcast([P, H, DH])).then_inc(bv_ld, 16)
            act.dma_start(rows_in[0:E * NF, :], b1.rearrange("e (k p) -> (e k) p", p=P)).then_inc(rows_ld, 16)
            act.dma_start(rows_in[E * NF:E * NF + E, :], b2).then_inc(rows_ld, 16)
            act.dma_start(rows_in[NCOL - 2:NCOL - 1, :], bq.unsqueeze(0)).then_inc(rows_ld, 16)
            act.dma_start(rows_in[NCOL - 1:NCOL, :].rearrange("o (h d) -> o h d", h=H),
                          bkv_v[0].unsqueeze(0)).then_inc(rows_ld, 16)
            act.sem_inc(gelu_done, NF)
            act.sem_inc(pt_moved, NG)
            act.sem_inc(cwb_moved, 1)
            act.wait_ge(pre_mm, J_W + 1)
            nc.scalar.activation(wT[:, 0, :], bank(J_W)[:, 0:P], ACT.Copy)
            nc.scalar.activation(wT[0:C, 1:3, :], bank(J_W)[0:C, P:3 * P].rearrange("p (a b) -> p a b", a=2), ACT.Copy)
            nc.scalar.activation(wT[:, 3, :], bank(J_W)[:, 3 * P:4 * P], ACT.Copy).then_inc(pre_act, 1)
            act.wait_ge(pre_mm, J_CTX + 1)
            nc.scalar.activation(cols[:, :], COLS, ACT.Copy).then_inc(cols_ready, 1)
            act.wait_ge(cols_ready, 1)
            for c in range(BG):
                act.wait_ge(pre_mm, J_CTX + c + 1)
                nc.scalar.activation(ctxT[:, TC * M * c:TC * M * (c + 1)], bank(J_CTX + c)[0:C, 0:TC * M],
                                     ACT.Copy).then_inc(pre_act, 1)
            act.wait_ge(c_ready, 6)
            nc.scalar.activation(pick[:, :], pick_f[:, :, :].rearrange("m h n -> m (h n)"),
                                 ACT.Copy).then_inc(pick_ready, 1)
            act.wait_ge(gates_ld, 32)
            nc.scalar.activation(tgates[:, :], gates[:, :], ACT.Tanh).then_inc(tg_ready, 1)
            for c in range(BG):
                act.wait_ge(pre_mm, J_XN + c + 1)
                nc.scalar.activation(xnT[:, CH * c:CH * (c + 1)], bank(J_XN + c), ACT.Copy).then_inc(pre_act, 1)
            act.wait_ge(pre_dve, BG)
            nc.scalar.activation(v_hi[:, :, :, :], v_sb[:, :, :, :], ACT.Copy).then_inc(v_split, 1)
            for c in range(BG):
                act.wait_ge(pre_mm, J_K + c + 1)
                nc.scalar.activation(kT[:, TC * M * c:TC * M * (c + 1)], bank(J_K + c)[:, 0:TC * M],
                                     ACT.Identity, bias=bk_c[:, 0:1]).then_inc(pre_act, 1)

            def move_pt(b, g):
                first, end = TG[g]
                act.wait_ge(pt_done, NG * b + g + 1)
                act.wait_ge(pv_done, NG * b + g + 1)
                nc.scalar.activation(probT[:, first:end, :], ps[:, TB + g % 2, 0:(end - first) * L]
                                     .rearrange("p (c l) -> p c l", l=L), ACT.Copy).then_inc(pt_moved, 1)

            def widen_rden(b):
                act.wait_ge(rden_done, b + 1)
                act.wait_ge(rT_done, b)
                nc.scalar.activation(rden_w[:, :].rearrange("p (h d) -> p h d", h=H), rden[:, :].unsqueeze(2).to_broadcast([P, H, DH]),
                                     ACT.Copy).then_inc(rw_done, 1)

            def move_rT(b):
                act.wait_ge(rT_done, b + 1)
                act.wait_ge(oT_ready, b)
                nc.scalar.activation(rT_sb[:, :], RT, ACT.Copy).then_inc(rT_moved, 1)

            def split_w(b):
                w = bass.ds(b * WS, WS)
                nc.scalar.activation(w1_hi[:, w], w1_in[:, w], ACT.Copy).then_inc(w_hi, 1)
                nc.scalar.activation(w2_hi[:, w], w2_in[:, w], ACT.Copy).then_inc(w_hi, 1)

            def exponentials(b, half, first=False):
                cols = slice(half * 2 * HM, (half + 1) * 2 * HM)
                act.wait_ge(sub_done, 2 * b + half + 1)
                if not first:
                    act.wait_ge(pt_done, NG * b)
                    act.wait_ge(den_done, b)
                nc.scalar.activation(prob[:, cols], shifted[:, :, :].rearrange("p q n -> p (q n)")[:, cols],
                                     ACT.Exp, scale=SCALE).then_inc(exp_done, 1)

            def stage_q(b, s, first=False):
                if not first:
                    act.wait_ge(scores_done, 2 * b - 2)
                for q in range(NQ):
                    rows = slice(32 * q, 32 * q + 32)
                    t = nc.scalar.activation(q_hi[rows, s, q, :], qT[rows, bass.ds(b * L, L)], ACT.Copy)
                t.then_inc(q_hi_done, 1)

            def attend(b, s, first=False, scores=True, queries=True):
                if queries:
                    stage_q(b + 2, s)
                split_w(b)
                if not first:
                    move_rT(b - 1)
                for g in range(NG):
                    move_pt(b, g)
                widen_rden(b)
                if scores:
                    exponentials(b + 1, 0)
                    exponentials(b + 1, 1)

            assert TC >= 2
            act.wait_ge(q_zero, 2)
            for c in range(BG):
                act.wait_ge(pre_mm, J_Q + c + 1)
                nc.scalar.activation(qT[:, CH * c:CH * (c + 1)], bank(J_Q + c),
                                     ACT.Identity, bias=bq_c[:, 0:1]).then_inc(pre_act, 1)
                if c == 0:
                    moved(act, J_Q)
                    stage_q(0, 0, first=True)
                    stage_q(1, 1, first=True)
            moved(act, J_Q + BG - 1)
            act.wait_ge(moe_ld, 16 * 3)
            exponentials(0, 0, first=True)
            exponentials(0, 1, first=True)
            attend(0, 0, first=True)
            attend(1, 1)
            with act.Fori(1, B // 2 - 1) as j:
                attend(2 * j, 0)
                attend(2 * j + 1, 1)
            attend(B - 2, 0, queries=False)
            attend(B - 1, 1, scores=False, queries=False)
            move_rT(B - 1)

            def move_cur(c):
                act.wait_ge(curT_done, c + 1)
                nc.scalar.activation(cur[:, CH * c:CH * (c + 1)], ps[:, CURT[c], :], ACT.Copy).then_inc(cur_ready, TC)

            for c in range(NC - 1):
                move_cur(c)

            def gelu(n, e, k):
                act.wait_ge(w1_done, n + 1)
                act.wait_ge(lo_done, n + 1)
                nc.scalar.activation(g_sb[:, k, :], ps[:, k, :], ACT.Gelu_apprx_tanh,
                                     bias=b1_c[:, e * NF + k:e * NF + k + 1]).then_inc(gelu_done, 1)

            def high(n, u, e, k):
                act.wait_ge(gelu_done, n + NF + 1)
                act.wait_ge(y_done, u + 1)
                nc.scalar.activation(h_hi[:, e % 2, k, :], g_sb[:, k, :], ACT.Copy).then_inc(hi_act, 1)

            def hidden(u, e, gate=None, first=False):
                n = u * NF
                gelu(n, e, 0)
                gelu(n + 1, e, 1)
                high(n + 1, u, e, 1)
                if first:
                    move_cur(NC - 1)
                if gate is not None:
                    act.wait_ge(gate_step, GATE_OPS * (gate + 1))
                    nc.scalar.activation(th[:, :, :], half_d[:, :, :], ACT.Tanh).then_inc(th_done, 1)
                gelu(n + 2, e, 2)
                gelu(n + 3, e, 3)
                high(n + 3, u, e, 3)

            def move_cwT(i):
                act.wait_ge(cwT_done, i + 1)
                act.wait_ge(cwb_done, E * i)
                nc.scalar.activation(cwT[:, :], CWB[0:CP * E, :], ACT.Copy).then_inc(cwT_moved, 1)

            def move_cwb(u, e):
                act.wait_ge(cwb_done, u + 1)
                act.wait_ge(y_read, u + 1)
                nc.scalar.activation(cwb_sb[:, e % 2, :], CWB, ACT.Copy).then_inc(cwb_moved, 1)

            hidden(0, 0, gate=0, first=True)
            with act.Fori(0, STEPS - 1) as i:
                for e in range(E):
                    u = i * E + e
                    hidden(u + 1, (e + 1) % E, gate=i + 1 if e == E - 1 else None)
                    if e == 0:
                        move_cwT(i)
                    move_cwb(u, e)
            for e in range(E):
                u = (STEPS - 1) * E + e
                if e < E - 1:
                    hidden(u + 1, e + 1)
                if e == 0:
                    move_cwT(STEPS - 1)
                move_cwb(u, e)

        @block.vector
        def _(dve):
            dve.sem_inc(lo_done, NF)
            dve.sem_inc(y_read, 2)
            nc.vector.memset(v_blk[:, PT - 1, :, :], 0.0).then_inc(fill_done, 1)
            nc.vector.memset(v_st[:, :, :], 0.0).then_inc(fill_done, 1)

            def moments(src, norm, c):
                for b in range(TC * c, TC * (c + 1)):
                    nc.vector.bn_stats(stats[:, b, :], src[:, b, :]).then_inc(bn_step, 1)
                dve.wait_ge(bn_step, norm * B + TC * (c + 1))
                for b in range(TC * c, TC * (c + 1)):
                    nc.vector.bn_aggr(mv[:, b, :], stats[:, b, :]).then_inc(mv_ready, 1)

            def normalise(src, norm, c):
                dve.wait_ge(rstd_ready, norm * NC + c + 1)
                for b in range(TC * c, TC * (c + 1)):
                    nc.vector.tensor_scalar(xn[:, b, :], src[:, b, :], mv[:, b, 0:1], rstd[:, b:b + 1],
                                            ALU.subtract, ALU.mult).then_inc(xn_ready, 1)

            nc.vector.memset(q_hi[:, :, :, :].bitcast(F32), 0.0).then_inc(q_zero, 1)
            nc.vector.memset(q_lo[:, :, :, :].bitcast(F32), 0.0).then_inc(q_zero, 1)

            def stage_q(b, s):
                dve.wait_ge(q_hi_done, b + 1)
                for q in range(NQ):
                    rows = slice(32 * q, 32 * q + 32)
                    t = nc.vector.tensor_tensor(q_lo[rows, s, q, :], qT[rows, bass.ds(b * L, L)],
                                                q_hi[rows, s, q, :].bitcast(F32), ALU.subtract)
                t.then_inc(q_lo_done, 1)

            for c in range(NC):
                dve.wait_ge(x_in[c], 16)
                moments(x_sb, 0, c)
            dve.wait_ge(c_ready, 6)
            nc.vector.tensor_reduce(head_mask[:, :], head_at[:, :, :].rearrange("p q h -> p h q"), AX.X,
                                    ALU.add).then_inc(headmask_ready, 1)
            for c in range(NC):
                normalise(x_sb, 0, c)
            dve.wait_ge(bv_ld, 16)
            for c in range(BG):
                dve.wait_ge(pre_mm, J_V + c + 1)
                nc.vector.tensor_tensor(
                    v_sb[:, TC * c:TC * (c + 1), :, :],
                    bank(J_V + c)[0:M, :].rearrange("m (b h d) -> m b h d", b=TC, h=H),
                    bv_row[0:M, :].rearrange("m (h d) -> m h d", h=H).unsqueeze(1).to_broadcast([M, TC, H, DH]),
                    ALU.add).then_inc(pre_dve, 1)
            dve.wait_ge(v_split, 1)
            nc.vector.tensor_tensor(v_lo[:, :, :, :], v_sb[:, :, :, :], v_hi[:, :, :, :].bitcast(F32),
                                    ALU.subtract).then_inc(v_split, 1)
            dve.wait_ge(fill_done, 1)
            for c in range(PT):
                n, h, k = tiles[c], head0[c], heads[c]
                dve.wait_ge(pre_mm, J_VF + c + 1)
                nc.vector.tensor_tensor(
                    v_blk[0:n, slot(c), :, 0:k * DH].rearrange("p b (h v) -> p b h v", v=DH),
                    bank(J_VF + c)[0:n, 0:B * k * DH].rearrange("p (b h v) -> p b h v", b=B, v=DH),
                    row_head[0:n, c, h:h + k].unsqueeze(1).unsqueeze(3).to_broadcast([n, B, k, DH]),
                    ALU.mult).then_inc(pre_dve, 1)
                if J_VF + c == SC_FREE:
                    moved(dve, J_Q)
                    dve.wait_ge(q_zero, 2)
                    stage_q(0, 0)
            stage_q(1, 1)
            dve.wait_ge(moe_ld, 16 * 3)
            nc.vector.tensor_copy(wg_s[:, :, 0, :], wg_in[:, :, :]).then_inc(wg_split, 1)
            dve.wait_ge(wg_split, 1)
            nc.vector.tensor_tensor(wg_s[:, :, 1, :], wg_in[:, :, :], wg_s[:, :, 0, :].bitcast(F32),
                                    ALU.subtract).then_inc(wg_split, 1)


            mx_v = mx[:, :].rearrange("p (q h) -> p q h", q=NQ)

            def shift(b, half, first=False):
                two = slice(2 * half, 2 * half + 2)
                scores = ps[:, SC + 2 * half:SC + 2 * half + 2, 0:HM].rearrange("p q (h m) -> p q h m", m=M)
                dve.wait_ge(scores_done, 2 * b + half + 1)
                nc.vector.tensor_reduce(mx_v[:, two, :], scores, AX.X, ALU.max).then_inc(mx_done, 1)
                dve.wait_ge(mx_done, 2 * b + half + 1)
                if not first:
                    dve.wait_ge(exp_done, 2 * b + half - 1)
                nc.vector.tensor_tensor(shifted[:, two, :].rearrange("p q (h m) -> p q h m", m=M), scores,
                                        mx_v[:, two, :].unsqueeze(3).to_broadcast([P, 2, HQ, M]),
                                        ALU.subtract).then_inc(sub_done, 1)

            def denominators(b):
                dve.wait_ge(exp_done, 2 * b + 2)
                nc.vector.tensor_reduce(den[:, :], prob[:, :].rearrange("p (h m) -> p h m", m=M), AX.X,
                                        ALU.add).then_inc(den_done, 1)
                dve.wait_ge(den_done, b + 1)
                dve.wait_ge(rw_done, b)
                nc.vector.reciprocal(rden[:, :], den[:, :]).then_inc(rden_done, 1)

            def normalise_o(b):
                dve.wait_ge(pv_done, NG * b + 2 * NG)
                dve.wait_ge(rT_moved, b + 1)
                dve.wait_ge(wo_done, b)
                nc.vector.tensor_tensor(oT_sb[:, :], OT, rT_sb[:, :], ALU.mult).then_inc(oT_ready, 1)

            def add_residual(b):
                row = bass.ds(b * D, D)
                dve.wait_ge(wo_done, b + 1)
                nc.vector.scalar_tensor_tensor(out=x1_sb[:, :, :].rearrange("p b d -> p (b d)")[:, row], in0=AO,
                                               scalar=tgates[:, 0:1],
                                               in1=xres[:, :, :].rearrange("p b d -> p (b d)")[:, row],
                                               op0=ALU.mult, op1=ALU.add).then_inc(x1_done, 1)

            def attend(b, s, scores=True, queries=True, values=True, residual=True, sums=True):
                if scores:
                    shift(b + 1, 0)
                if queries:
                    stage_q(b + 2, s)
                if sums:
                    denominators(b)
                if scores:
                    shift(b + 1, 1)
                if residual:
                    add_residual(b - 2)
                if values:
                    normalise_o(b - 1)

            moved(dve, JOBS - 1)
            dve.wait_ge(xres_step, 2)
            shift(0, 0, first=True)
            shift(0, 1, first=True)
            attend(0, 0, values=False, residual=False)
            attend(1, 1, residual=False)
            with dve.Fori(1, B // 2 - 1) as j:
                attend(2 * j, 0)
                attend(2 * j + 1, 1)
            attend(B - 2, 0, queries=False)
            attend(B - 1, 1, scores=False, queries=False)

            for c in range(NC - 1):
                dve.wait_ge(x1_done, TC * (c + 1))
                moments(x1_sb, 1, c)
            normalise(x1_sb, 1, 0)
            attend(B, 0, scores=False, queries=False, sums=False)
            normalise(x1_sb, 1, 1)
            add_residual(B - 1)
            dve.wait_ge(x1_done, B)
            moments(x1_sb, 1, NC - 1)
            normalise(x1_sb, 1, 2)

            def split_x(i):
                cc = cur[:, bass.ds((i % NC) * CH, CH)]
                dve.wait_ge(cur_ready, TC * i + TC)
                dve.wait_ge(w1_done, E * NF * i)
                nc.vector.tensor_copy(x_hi[:, :], cc).then_inc(x_hi_done, 1)
                dve.wait_ge(x_hi_done, i + 1)
                nc.vector.tensor_tensor(x_lo[:, :], cc, x_hi[:, :].bitcast(F32), ALU.subtract).then_inc(x_split, 1)

            def lo(n, e, k):
                nc.vector.tensor_tensor(h_lo[:, e % 2, k, :], g_sb[:, k, :],
                                        h_hi[:, e % 2, k, :].bitcast(F32), ALU.subtract).then_inc(lo_done, 1)

            def split_hidden(u, e, pair):
                k = 2 * pair
                n = u * NF + k
                dve.wait_ge(gelu_done, n + NF + 1)
                dve.wait_ge(y_done, u + 1)
                nc.vector.tensor_copy(h_hi[:, e % 2, k, :], g_sb[:, k, :]).then_inc(hi_dve, 1)
                dve.wait_ge(hi_dve, 2 * u + pair + 1)
                lo(n, e, k)
                dve.wait_ge(hi_act, 2 * u + pair + 1)
                lo(n + 1, e, k + 1)

            def share(u, e):
                dve.wait_ge(y_done, u + 3)
                dve.wait_ge(cwb_moved, u + 2)
                dve.wait_ge(cur_ready, B + u - 1)
                nc.vector.scalar_tensor_tensor(out=contrib[:, e % 2, :], in0=ps[:, YB + e % 2, :],
                                               scalar=b2_c[:, e:e + 1], in1=cwb_sb[:, e % 2, :],
                                               op0=ALU.add, op1=ALU.mult).then_inc(y_read, 1)

            def router(i):
                t = [GATE_OPS * i]

                def step(ins):
                    t[0] = t[0] + 1
                    ins.then_inc(gate_step, 1)

                def settle():
                    dve.wait_ge(gate_step, t[0])

                r = i // NC
                bgr = bg_row[:, bass.ds(r * E, E)].unsqueeze(1).to_broadcast([P, TC, E])
                lg_v = LG.rearrange("p (t n) -> p t n", t=TC)
                dve.wait_ge(logits_done, i + 1)
                step(nc.vector.tensor_tensor(lga[:, :, :], lg_v[:, :, bass.ds(r * (2 * E), E)], bgr, ALU.add))
                settle()
                step(nc.vector.tensor_tensor(lg[:, :, :], lg_v[:, :, bass.ds(r * (2 * E) + E, E)],
                                             lga[:, :, :], ALU.add))
                settle()
                other = lg[:, :, :].unsqueeze(2).to_broadcast([P, TC, E, E])
                mine = lg[:, :, :].unsqueeze(3).to_broadcast([P, TC, E, E])
                step(nc.vector.tensor_tensor(beat_ge[:, :, :, :], other, mine, ALU.is_ge))
                step(nc.vector.tensor_tensor(beat_gt[:, :, :, :], other, mine, ALU.is_gt))
                settle()
                step(nc.vector.tensor_tensor(beat_ge[:, :, :, :], beat_ge[:, :, :, :],
                                             before[:, :, :].unsqueeze(1).to_broadcast([P, TC, E, E]), ALU.mult))
                step(nc.vector.tensor_tensor(beat_gt[:, :, :, :], beat_gt[:, :, :, :],
                                             after[:, :, :].unsqueeze(1).to_broadcast([P, TC, E, E]), ALU.mult))
                settle()
                step(nc.vector.tensor_tensor(beat_ge[:, :, :, :], beat_ge[:, :, :, :], beat_gt[:, :, :, :], ALU.add))
                settle()
                step(nc.vector.tensor_reduce(rank[:, :, :], beat_ge[:, :, :, :], AX.X, ALU.add))
                settle()
                step(nc.vector.scalar_tensor_tensor(out=sel_lg[:, :, :], in0=rank[:, :, :], scalar=2.0,
                                                    in1=lg[:, :, :], op0=ALU.is_lt, op1=ALU.mult))
                settle()
                step(nc.vector.tensor_reduce(sel_sum[:, :], sel_lg[:, :, :], AX.X, ALU.add))
                settle()
                step(nc.vector.scalar_tensor_tensor(out=half_d[:, :, :],
                                                    in0=sel_sum[:, :].unsqueeze(2).to_broadcast([P, TC, E]),
                                                    scalar=-0.5, in1=lg[:, :, :], op0=ALU.mult, op1=ALU.add))

            def weights(i):
                dve.wait_ge(th_done, i + 1)
                nc.vector.tensor_scalar(wgt[:, :, :], th[:, :, :], 0.5, 0.5, ALU.mult,
                                        ALU.add).then_inc(wgt_done, 1)
                dve.wait_ge(wgt_done, i + 1)
                nc.vector.scalar_tensor_tensor(out=cw[:, :, :], in0=rank[:, :, :], scalar=2.0,
                                               in1=wgt[:, :, :], op0=ALU.is_lt, op1=ALU.mult).then_inc(cw_step, 1)
                dve.wait_ge(cwT_done, i)
                dve.wait_ge(cw_step, 4 * i + 1)
                nc.vector.tensor_copy(cw_parts[:, :, 0, :], cw[:, :, :]).then_inc(cw_step, 1)
                dve.wait_ge(cw_step, 4 * i + 2)
                nc.vector.tensor_tensor(cw_rest[:, :, :], cw[:, :, :], cw_parts[:, :, 0, :],
                                        ALU.subtract).then_inc(cw_step, 1)
                dve.wait_ge(cw_step, 4 * i + 3)
                nc.vector.tensor_copy(cw_parts[:, :, 1, :], cw_rest[:, :, :]).then_inc(cw_step, 1)
                dve.wait_ge(cw_step, 4 * i + 4)
                nc.vector.tensor_tensor(cw_parts[:, :, 2, :], cw_rest[:, :, :], cw_parts[:, :, 1, :],
                                        ALU.subtract).then_inc(cw_ready, 1)

            def unit(i, e, last=False):
                u = i * E + e
                if e == E - 1 and not last:
                    router(i + 1)
                if not (last and e == E - 1):
                    split_hidden(u + 1, (e + 1) % E, 0)
                    if e == E - 2 and not last:
                        split_x(i + 1)
                    split_hidden(u + 1, (e + 1) % E, 1)
                if e == E - 1 and not last:
                    weights(i + 1)
                share(u, e)

            split_x(0)
            normalise(x1_sb, 1, NC - 1)
            router(0)
            split_hidden(0, 0, 0)
            split_hidden(0, 0, 1)
            weights(0)
            with dve.Fori(0, STEPS - 1) as i:
                for e in range(E):
                    unit(i, e)
            for e in range(E):
                unit(STEPS - 1, e, last=True)

            for c in range(NC):
                dve.wait_ge(fin_mm, c + 1)
                nc.vector.scalar_tensor_tensor(
                    out=out_sb[:, TC * c:TC * (c + 1), :], in0=ps[:, c, :].rearrange("p (b d) -> p b d", b=TC),
                    scalar=tgates[:, 1:2], in1=x1_sb[:, TC * c:TC * (c + 1), :],
                    op0=ALU.mult, op1=ALU.add).then_inc(fin_done, 1)

        @block.tensor
        def _(pe):
            pe.sem_inc(pv_done, NG)
            pe.sem_inc(y_done, 2)
            mm = nc.tensor.matmul
            tr = nc.tensor.transpose
            pe.wait_ge(c_ready, 1)
            pe.wait_ge(wproj_ld, 16 * 4)
            tr(bank(J_W)[:, 0:P], wq_in[:, :], ident[:, :])
            tr(bank(J_W)[0:C, P:2 * P], wk_in[:, :], ident[:, :])
            tr(bank(J_W)[0:C, 2 * P:3 * P], wv_in[:, :], ident[:, :])
            tr(bank(J_W)[:, 3 * P:4 * P], wo_in[:, :], ident[:, :]).then_inc(pre_mm, 1)
            pe.wait_ge(rows_ld, 16 * 4)
            tr(COLS, rows_in[:, :], ident[0:NCOL, 0:NCOL])
            pe.wait_ge(ctx_ld, 16)
            for b in range(B):
                j = J_CTX + b // TC
                t = tr(bank(j)[0:C, (b % TC) * M:(b % TC + 1) * M], ctx_sb[:, b, :], ident[0:M, 0:M])
                if b % TC == TC - 1:
                    t.then_inc(pre_mm, 1)
            moved(pe, J_W)
            for b in range(B):
                j = J_V + b // TC
                if b % TC == 0:
                    moved(pe, J_CTX + b // TC)
                    if j >= 8:
                        moved(pe, j - 8)
                t = mm(bank(j)[0:M, (b % TC) * D:(b % TC + 1) * D], ctxT[:, b * M:(b + 1) * M], wT[0:C, 2, :],
                       start=True, stop=True)
                if b % TC == TC - 1:
                    t.then_inc(pre_mm, 1)
            for b in range(B):
                j = J_XN + b // TC
                if b % TC == 0:
                    moved(pe, j - 8)
                pe.wait_ge(xn_ready, b + 1)
                t = tr(bank(j)[:, (b % TC) * L:(b % TC + 1) * L], xn[:, b, :], ident[:, :])
                if b % TC == TC - 1:
                    t.then_inc(pre_mm, 1)
            for c in range(BG):
                moved(pe, J_K + c - 8)
                mm(bank(J_K + c)[:, 0:TC * M], wT[0:C, 1, :], ctxT[:, TC * M * c:TC * M * (c + 1)],
                   start=True, stop=True).then_inc(pre_mm, 1)
            for c in range(BG):
                j = J_Q + c
                moved(pe, j - 8)
                moved(pe, J_XN + c)
                mm(bank(j), wT[:, 0, :], xnT[:, CH * c:CH * (c + 1)], start=True, stop=True).then_inc(pre_mm, 1)

            pe.wait_ge(v_split, 2)
            pe.wait_ge(pick_ready, 1)
            for c in range(PT):
                j = J_VF + c
                n, h = tiles[c], slice(head0[c], head0[c] + heads[c])
                moved(pe, j - 8)
                for m, v in enumerate((v_hi, v_lo)):
                    t = mm(bank(j)[0:n, 0:B * heads[c] * DH].rearrange("p (b x) -> p b x", b=B), pick[:, P * c:P * c + n],
                           v[:, :, h, :].rearrange("m b h v -> m b (h v)"), start=m == 0, stop=m == 1)
                t.then_inc(pre_mm, 1)

            def scores(b, s, q, first=False):
                if q == 0:
                    pe.wait_ge(q_lo_done, b + 1)
                    pe.wait_ge(k_stage, 3 * b + 3)
                if q % 2 == 0 and not first:
                    pe.wait_ge(sub_done, 2 * b - 1 + q // 2)
                passes = ((q_hi, k_hi), (q_hi, k_lo), (q_lo, k_hi))
                for n, (qs, ks) in enumerate(passes):
                    t = mm(ps[:, SC + q, 0:HM], qs[:, s, q, :], ks[:, s, :], start=n == 0, stop=n == len(passes) - 1)
                if q % 2 == 1:
                    t.then_inc(scores_done, 1)

            def transpose_probs(b, g):
                pe.wait_ge(exp_done, 2 * b + (1 if TG[g][1] * P <= 2 * HM else 2))
                pe.wait_ge(pt_moved, NG * b + NG + (1 if g == 2 else 0))
                for k, c in enumerate(range(*TG[g])):
                    t = tr(ps[0:tiles[c], TB + g % 2, k * L:(k + 1) * L], prob[:, P * c:P * c + tiles[c]], ident[:, :])
                t.then_inc(pt_done, 1)

            def weigh_values(b, s, first, end):
                if first == 0 and end > 0:
                    pe.wait_ge(v_stage, 2 * b + 2)
                    pe.wait_ge(oT_ready, b)
                for c in range(first, end):
                    for g, tg in enumerate(TG):
                        if c == tg[0]:
                            pe.wait_ge(pt_moved, NG * b + g + NG + 1)
                    n = tiles[c]
                    t = mm(OT, v_st[0:n, s, c * P:(c + 1) * P], probT[0:n, c, :], start=c == 0, stop=c == PT - 1)
                    if any(c == tg[1] - 1 for tg in TG):
                        t.then_inc(pv_done, 1)

            def transpose_rden(b, first=False):
                pe.wait_ge(rw_done, b + 1)
                if not first:
                    pe.wait_ge(x1_done, b - 1)
                    pe.wait_ge(rT_moved, b)
                tr(RT, rden_w[:, :], ident[:, :]).then_inc(rT_done, 1)

            def project_o(b, last=False):
                pe.wait_ge(oT_ready, b + 1)
                if not last:
                    pe.wait_ge(rT_moved, b + 2)
                if last:
                    pe.wait_ge(x1_done, b)
                mm(AO, oT_sb[:, :], wT[:, 3, :], start=True, stop=True).then_inc(wo_done, 1)

            def attend(b, s, logits=True, values=True, project=True, probs=True):
                for q in range(NQ):
                    if logits:
                        scores(b + 1, 1 - s, q)
                    if q == 2 and project:
                        project_o(b - 2)
                    if values:
                        weigh_values(b - 1, 1 - s, *PVS[q])
                    if q == 1 and values:
                        transpose_rden(b - 1, first=not project)
                if probs:
                    for g in range(NG):
                        transpose_probs(b, g)

            moved(pe, SC_FREE)
            for q in range(NQ):
                scores(0, 0, q, first=True)
            moved(pe, JOBS - 1)
            attend(0, 0, values=False, project=False)
            attend(1, 1, project=False)
            with pe.Fori(1, B // 2 - 1) as j:
                attend(2 * j, 0)
                attend(2 * j + 1, 1)
            attend(B - 2, 0)
            attend(B - 1, 1, logits=False)
            attend(B, 0, logits=False, probs=False)

            def transpose_x(c):
                if c < 2:
                    pe.wait_ge(pt_moved, NG * (B + 1))
                for t in range(TC):
                    b = TC * c + t
                    pe.wait_ge(xn_ready, B + b + 1)
                    m = tr(ps[:, CURT[c], t * L:(t + 1) * L], xn[:, b, :], ident[:, :])
                m.then_inc(curT_done, 1)

            transpose_x(0)
            project_o(B - 1, last=True)
            transpose_x(1)
            transpose_x(2)

            def logits(i):
                pe.wait_ge(x_split, i + 1)
                pe.wait_ge(gate_step, GATE_OPS * i)
                for t in range(TC):
                    o = LG[:, t * LG_N:(t + 1) * LG_N]
                    wg = wg_s[:, :, :, :].rearrange("p r s e -> p (r s e)")
                    mm(o, x_hi[:, t * P:(t + 1) * P], wg, start=True, stop=False)
                    m = mm(o, x_lo[:, t * P:(t + 1) * P], wg, start=False, stop=True)
                m.then_inc(logits_done, 1)

            def up(u, e):
                for k in range(NF):
                    n = u * NF + k
                    w = slice(e * F + k * P, e * F + (k + 1) * P)
                    pe.wait_ge(gelu_done, n + 1)
                    mm(ps[:, k, :], w1_hi[:, w], x_hi[:, :], start=True, stop=False)
                    mm(ps[:, k, :], w1_hi[:, w], x_lo[:, :], start=False, stop=False)
                    mm(ps[:, k, :], w1_lo[:, w], x_hi[:, :], start=False, stop=True).then_inc(w1_done, 1)

            def transpose_weights(i):
                pe.wait_ge(cw_ready, i + 1)
                pe.wait_ge(cwb_moved, E * i + 1)
                for t in range(TC):
                    m = mm(CWB[0:CP * E, t * P:(t + 1) * P], cw_parts[:, t, :, :].rearrange("p c e -> p (c e)"),
                           ident_b[:, :], start=True, stop=True)
                m.then_inc(cwT_done, 1)

            def spread(u, i, e):
                if e == 0:
                    pe.wait_ge(cwT_moved, i + 1)
                pe.wait_ge(cwb_moved, u + 1)
                mm(CWB, spread_by[:, e, :], cwT[:, :], start=True, stop=True).then_inc(cwb_done, 1)

            def down(u, e):
                pe.wait_ge(y_read, u + 1)
                yb = ps[:, YB + e % 2, :]
                for k in range(NF):
                    w = slice((e * NF + k) * D, (e * NF + k + 1) * D)
                    pe.wait_ge(lo_done, u * NF + k + NF + 1)
                    hh, hl = h_hi[:, e % 2, k, :], h_lo[:, e % 2, k, :]
                    mm(yb, w2_hi[:, w], hh, start=k == 0, stop=False)
                    mm(yb, w2_hi[:, w], hl, start=False, stop=False)
                    m = mm(yb, w2_lo[:, w], hh, start=False, stop=k == NF - 1)
                m.then_inc(y_done, 1)

            def combine(u, i, e):
                if e == 0:
                    transpose_weights(i)
                    down(u, e)
                    spread(u, i, e)
                else:
                    spread(u, i, e)
                    down(u, e)

            pe.wait_ge(wg_split, 2)
            pe.wait_ge(w_split, 2 * B)
            pe.wait_ge(x1_done, B)
            pe.wait_ge(sub_done, 2 * B)
            logits(0)
            up(0, 0)
            pe.wait_ge(cur_ready, TC)
            transpose_x(NC - 1)
            pe.wait_ge(cur_ready, B)
            pe.wait_ge(spread_ready, 2)
            with pe.Fori(0, STEPS - 1) as i:
                for e in range(E):
                    u = i * E + e
                    if e == E - 1:
                        logits(i + 1)
                    up(u + 1, (e + 1) % E)
                    combine(u, i, e)
            for e in range(E):
                u = (STEPS - 1) * E + e
                if e < E - 1:
                    up(u + 1, e + 1)
                combine(u, STEPS - 1, e)

            for c in range(NC):
                pe.wait_ge(cur_ready, B + E * (STEPS - NC + c + 1))
                for t in range(TC):
                    b = c * TC + t
                    m = tr(ps[:, c, t * P:(t + 1) * P], cur[:, b * P:(b + 1) * P], ident[:, :])
                m.then_inc(fin_mm, 1)


_INS = ["x", "ctx_768", "g_xattn", "g_ffn", "L0_xattn_Wq", "L0_xattn_bq", "L0_xattn_Wkv", "L0_xattn_bkv",
        "L0_xattn_Wo", "L0_xattn_bo", "L0_ffn_Wg", "L0_ffn_bg", "L0_ffn_W1", "L0_ffn_b1", "L0_ffn_W2", "L0_ffn_b2"]


def kernel(**inputs):
    import numpy as _np
    import concourse.bacc as _bacc
    from concourse import mybir as _mybir
    from concourse.bass_utils import run_bass_kernel_spmd as _run

    nc = _bacc.Bacc("TRN2", target_bir_lowering=False, num_devices=1)
    arrays, args = {}, []
    for name in _INS:
        a = _np.ascontiguousarray(inputs[name])
        arrays[f"in_{name}_dram"] = a
        args.append(nc.dram_tensor(f"in_{name}_dram", a.shape, _mybir.dt.from_np(a.dtype), kind="ExternalInput").ap())
    x = inputs["x"]
    args.append(nc.dram_tensor("out_0_dram", x.shape, _mybir.dt.float32, kind="ExternalOutput").ap())
    flamingo_gated_block(nc, *args)
    r = _run(nc, [arrays], core_ids=[0])
    return r.results[0]["out_0_dram"]
```
